# Optimizing a Trainium2 kernel written in Bass

```python
import numpy as np
import jax
import jax.numpy as jnp

def _softmax(x, axis=-1):
    return jax.nn.softmax(x, axis=axis)

def _gelu(x):
    return jax.nn.gelu(x, approximate=True)

def _silu(x):
    return jax.nn.silu(x)

def _sigmoid(x):
    return jax.nn.sigmoid(x)

def _layernorm(x, axis=-1, eps=1e-05):
    m = jnp.mean(x, axis=axis, keepdims=True)
    v = jnp.var(x, axis=axis, keepdims=True)
    return (x - m) / jnp.sqrt(v + eps)

def _scatter_add(tgt, idx, src, axis=0):
    return tgt.at[idx].add(src)

def _segment_sum(src, seg, n):
    return jax.ops.segment_sum(src, seg, n)
kernel_name = 'mk_prb_d1_jaxref_r4_03d047'

def setup_inputs(seed: int=0):
    np.random.seed(seed)
    _w = jnp.asarray

    def _L0_attn_setup():
        import math
        import jax, jax.numpy as jnp
        import numpy as np
        D_MODEL = 256
        D_STATE = 16
        D_CONV = 4
        EXPAND = 2
        D_INNER = D_MODEL * EXPAND
        B_SZ = 2
        L_SEQ = 512
        DT_MIN = 0.001
        DT_MAX = 0.1

        def _silu(v):
            return v * jax.nn.sigmoid(v)

        def _mamba(x, in_proj_w, conv_w, conv_b, x_proj_w, dt_proj_w, dt_proj_b, A_log, D, out_proj_w):
            xz = jnp.einsum('bld,ed->ble', x, in_proj_w)
            x_in, z = jnp.split(xz, 2, axis=-1)
            xc = jnp.swapaxes(x_in, 1, 2)
            xc = jax.lax.conv_general_dilated(xc, conv_w, window_strides=(1,), padding=[(D_CONV - 1, 0)], dimension_numbers=('NCH', 'OIH', 'NCH'), feature_group_count=D_INNER)
            xc = xc + conv_b[None, :, None]
            x_in = _silu(jnp.swapaxes(xc, 1, 2))
            dbc = jnp.einsum('bld,ed->ble', x_in, x_proj_w)
            delta_in = dbc[..., :D_INNER]
            Bp = dbc[..., D_INNER:D_INNER + D_STATE]
            Cp = dbc[..., D_INNER + D_STATE:]
            delta = jax.nn.softplus(jnp.einsum('bld,ed->ble', delta_in, dt_proj_w) + dt_proj_b)
            A = -jnp.exp(A_log)

            def step(h, inp):
                dt, bt, ct, xt = inp
                dA = jnp.exp(dt[:, :, None] * A[None])
                h = dA * h + dt[:, :, None] * bt[:, None, :] * xt[:, :, None]
                y = jnp.einsum('bds,bs->bd', h, ct) + D * xt
                return (h, y)
            tm = lambda a: jnp.swapaxes(a, 0, 1)
            h0 = jnp.zeros((x.shape[0], D_INNER, D_STATE), x.dtype)
            _, y = jax.lax.scan(step, h0, (tm(delta), tm(Bp), tm(Cp), tm(x_in)))
            y = jnp.swapaxes(y, 0, 1)
            return jnp.einsum('ble,de->bld', y * _silu(z), out_proj_w)
        key = jax.random.key(seed)
        ks = jax.random.split(key, 8)

        def lin(k, out_f, in_f):
            return jax.random.normal(k, (out_f, in_f), jnp.float32) / np.sqrt(in_f)
        x = jax.random.normal(ks[0], (B_SZ, L_SEQ, D_MODEL), jnp.float32)
        in_proj_w = lin(ks[1], 2 * D_INNER, D_MODEL)
        conv_w = jax.random.normal(ks[2], (D_INNER, 1, D_CONV), jnp.float32) / np.sqrt(D_CONV)
        conv_b = jnp.zeros((D_INNER,), jnp.float32)
        x_proj_w = lin(ks[3], 2 * D_STATE + D_INNER, D_INNER)
        dt_proj_w = lin(ks[4], D_INNER, D_INNER)
        dt = jnp.exp(jax.random.uniform(ks[5], (D_INNER,), jnp.float32) * (math.log(DT_MAX) - math.log(DT_MIN)) + math.log(DT_MIN))
        dt_proj_b = dt + jnp.log(-jnp.expm1(-dt))
        A_log = jnp.log(jnp.tile(jnp.arange(1, D_STATE + 1, dtype=jnp.float32), (D_INNER, 1)))
        D = jnp.ones((D_INNER,), jnp.float32)
        out_proj_w = lin(ks[6], D_MODEL, D_INNER)
        return dict(x=x, in_proj_w=in_proj_w, conv_w=conv_w, conv_b=conv_b, x_proj_w=x_proj_w, dt_proj_w=dt_proj_w, dt_proj_b=dt_proj_b, A_log=A_log, D=D, out_proj_w=out_proj_w)
    _L0_attn_in = _L0_attn_setup()

    def _L0_ffn_setup():
        import jax, jax.numpy as jnp
        import numpy as np
        H, I, E, K = (256, 128, 32, 8)
        B, S = (4, 256)

        def silu(x):
            return x * jax.nn.sigmoid(x)
        key = jax.random.key(seed)
        ks = jax.random.split(key, 14)

        def w(k, shape, fan_in):
            return jax.random.normal(k, shape, jnp.float32) / np.float32(np.sqrt(fan_in))
        return {'hidden_states': jax.random.normal(ks[0], (B, S, H), jnp.float32), 'Wr': w(ks[1], (H, E), H), 'br': jnp.zeros((E,), jnp.float32), 'Wg_s': w(ks[2], (H, I), H), 'bg_s': jnp.zeros((I,), jnp.float32), 'Wu_s': w(ks[3], (H, I), H), 'bu_s': jnp.zeros((I,), jnp.float32), 'Wd_s': w(ks[4], (I, H), I), 'bd_s': jnp.zeros((H,), jnp.float32), 'Wg': w(ks[5], (E, H, I), H), 'bg': jnp.zeros((E, I), jnp.float32), 'Wu': w(ks[6], (E, H, I), H), 'bu': jnp.zeros((E, I), jnp.float32), 'Wd': w(ks[7], (E, I, H), I), 'bd': jnp.zeros((E, H), jnp.float32)}
    _L0_ffn_in = _L0_ffn_setup()
    _d = {'L0_attn_x': _L0_attn_in['x'], 'L0_attn_in_proj_w': _L0_attn_in['in_proj_w'], 'L0_attn_conv_w': _L0_attn_in['conv_w'], 'L0_attn_conv_b': _L0_attn_in['conv_b'], 'L0_attn_x_proj_w': _L0_attn_in['x_proj_w'], 'L0_attn_dt_proj_w': _L0_attn_in['dt_proj_w'], 'L0_attn_dt_proj_b': _L0_attn_in['dt_proj_b'], 'L0_attn_A_log': _L0_attn_in['A_log'], 'L0_attn_D': _L0_attn_in['D'], 'L0_attn_out_proj_w': _L0_attn_in['out_proj_w'], 'L0_ffn_Wr': _L0_ffn_in['Wr'], 'L0_ffn_br': _L0_ffn_in['br'], 'L0_ffn_Wg_s': _L0_ffn_in['Wg_s'], 'L0_ffn_bg_s': _L0_ffn_in['bg_s'], 'L0_ffn_Wu_s': _L0_ffn_in['Wu_s'], 'L0_ffn_bu_s': _L0_ffn_in['bu_s'], 'L0_ffn_Wd_s': _L0_ffn_in['Wd_s'], 'L0_ffn_bd_s': _L0_ffn_in['bd_s'], 'L0_ffn_Wg': _L0_ffn_in['Wg'], 'L0_ffn_bg': _L0_ffn_in['bg'], 'L0_ffn_Wu': _L0_ffn_in['Wu'], 'L0_ffn_bu': _L0_ffn_in['bu'], 'L0_ffn_Wd': _L0_ffn_in['Wd'], 'L0_ffn_bd': _L0_ffn_in['bd']}
    _x0 = _d['L0_attn_x']
    _d['L0_attn_x'] = jax.random.normal(jax.random.fold_in(jax.random.key(seed), 1), (4, 1024, 256), dtype=_x0.dtype)
    del _x0
    return _d

def reference(L0_attn_x, L0_attn_in_proj_w, L0_attn_conv_w, L0_attn_conv_b, L0_attn_x_proj_w, L0_attn_dt_proj_w, L0_attn_dt_proj_b, L0_attn_A_log, L0_attn_D, L0_attn_out_proj_w, L0_ffn_Wr, L0_ffn_br, L0_ffn_Wg_s, L0_ffn_bg_s, L0_ffn_Wu_s, L0_ffn_bu_s, L0_ffn_Wd_s, L0_ffn_bd_s, L0_ffn_Wg, L0_ffn_bg, L0_ffn_Wu, L0_ffn_bu, L0_ffn_Wd, L0_ffn_bd):

    def _L0_attn_ref(x, in_proj_w, conv_w, conv_b, x_proj_w, dt_proj_w, dt_proj_b, A_log, D, out_proj_w):
        import math
        import jax, jax.numpy as jnp
        import numpy as np
        D_MODEL = 256
        D_STATE = 16
        D_CONV = 4
        EXPAND = 2
        D_INNER = D_MODEL * EXPAND
        B_SZ = 2
        L_SEQ = 512
        DT_MIN = 0.001
        DT_MAX = 0.1

        def _silu(v):
            return v * jax.nn.sigmoid(v)

        def _mamba(x, in_proj_w, conv_w, conv_b, x_proj_w, dt_proj_w, dt_proj_b, A_log, D, out_proj_w):
            xz = jnp.einsum('bld,ed->ble', x, in_proj_w)
            x_in, z = jnp.split(xz, 2, axis=-1)
            xc = jnp.swapaxes(x_in, 1, 2)
            xc = jax.lax.conv_general_dilated(xc, conv_w, window_strides=(1,), padding=[(D_CONV - 1, 0)], dimension_numbers=('NCH', 'OIH', 'NCH'), feature_group_count=D_INNER)
            xc = xc + conv_b[None, :, None]
            x_in = _silu(jnp.swapaxes(xc, 1, 2))
            dbc = jnp.einsum('bld,ed->ble', x_in, x_proj_w)
            delta_in = dbc[..., :D_INNER]
            Bp = dbc[..., D_INNER:D_INNER + D_STATE]
            Cp = dbc[..., D_INNER + D_STATE:]
            delta = jax.nn.softplus(jnp.einsum('bld,ed->ble', delta_in, dt_proj_w) + dt_proj_b)
            A = -jnp.exp(A_log)

            def step(h, inp):
                dt, bt, ct, xt = inp
                dA = jnp.exp(dt[:, :, None] * A[None])
                h = dA * h + dt[:, :, None] * bt[:, None, :] * xt[:, :, None]
                y = jnp.einsum('bds,bs->bd', h, ct) + D * xt
                return (h, y)
            tm = lambda a: jnp.swapaxes(a, 0, 1)
            h0 = jnp.zeros((x.shape[0], D_INNER, D_STATE), x.dtype)
            _, y = jax.lax.scan(step, h0, (tm(delta), tm(Bp), tm(Cp), tm(x_in)))
            y = jnp.swapaxes(y, 0, 1)
            return jnp.einsum('ble,de->bld', y * _silu(z), out_proj_w)
        return _mamba(x, in_proj_w, conv_w, conv_b, x_proj_w, dt_proj_w, dt_proj_b, A_log, D, out_proj_w)

    def _L0_ffn_ref(hidden_states, Wr, br, Wg_s, bg_s, Wu_s, bu_s, Wd_s, bd_s, Wg, bg, Wu, bu, Wd, bd):
        import jax, jax.numpy as jnp
        import numpy as np
        H, I, E, K = (256, 128, 32, 8)
        B, S = (4, 256)

        def silu(x):
            return x * jax.nn.sigmoid(x)
        b, s, h = hidden_states.shape
        T = b * s
        x = hidden_states.reshape(T, h)
        logits = jnp.dot(x.astype(jnp.float32), Wr) + br
        aff = jax.nn.sigmoid(logits)
        top_v, top_i = jax.lax.top_k(aff, K)
        top_w = top_v / (jnp.sum(top_v, axis=-1, keepdims=True) + 1e-09)
        top_w = top_w.astype(hidden_states.dtype)
        e_total = Wr.shape[1]
        w_full = jnp.zeros((T, e_total), hidden_states.dtype)
        w_full = w_full.at[jnp.arange(T)[:, None], top_i].set(top_w)
        shared = jnp.dot(silu(jnp.dot(x, Wg_s) + bg_s) * (jnp.dot(x, Wu_s) + bu_s), Wd_s) + bd_s
        gate = silu(jnp.einsum('th,ehi->eti', x, Wg) + bg[:, None, :])
        up = jnp.einsum('th,ehi->eti', x, Wu) + bu[:, None, :]
        down = jnp.einsum('eti,eih->eth', gate * up, Wd) + bd[:, None, :]
        routed = jnp.einsum('te,eth->th', w_full, down)
        return (shared + routed).reshape(b, s, h)
    x = L0_attn_x
    xn = _layernorm(x, axis=-1)
    x = x + _L0_attn_ref(xn, L0_attn_in_proj_w, L0_attn_conv_w, L0_attn_conv_b, L0_attn_x_proj_w, L0_attn_dt_proj_w, L0_attn_dt_proj_b, L0_attn_A_log, L0_attn_D, L0_attn_out_proj_w) + _L0_ffn_ref(xn, L0_ffn_Wr, L0_ffn_br, L0_ffn_Wg_s, L0_ffn_bg_s, L0_ffn_Wu_s, L0_ffn_bu_s, L0_ffn_Wd_s, L0_ffn_bd_s, L0_ffn_Wg, L0_ffn_bg, L0_ffn_Wu, L0_ffn_bu, L0_ffn_Wd, L0_ffn_bd)
    return x

_drawn_inputs = setup_inputs


def setup_inputs(seed=0):
    import zlib

    import numpy as np

    out = dict(_drawn_inputs(seed))
    spreads = {'L0_attn_conv_b': (0.0, 0.1),
     'L0_attn_D': (1.0, 0.2),
     'L0_ffn_br': (0.0, 0.1),
     'L0_ffn_bg_s': (0.0, 0.1),
     'L0_ffn_bu_s': (0.0, 0.1),
     'L0_ffn_bd_s': (0.0, 0.1),
     'L0_ffn_bg': (0.0, 0.465),
     'L0_ffn_bu': (0.0, 0.477),
     'L0_ffn_bd': (0.0, 0.284)}
    factors = {}
    for name, (base, spread) in spreads.items():
        noise = np.random.default_rng([zlib.crc32(name.encode()), seed]).standard_normal(out[name].shape)
        drawn = base * np.exp(spread * noise) if base else spread * noise
        out[name] = jnp.asarray(drawn.astype(out[name].dtype))
    for name, factor in factors.items():
        out[name] = (out[name] * factor).astype(out[name].dtype)
    return out
```

```python
from contextlib import ExitStack

import concourse.bass as bass
from concourse import mybir

F32 = mybir.dt.float32
F32R = mybir.dt.float32r
ALU = mybir.AluOpType
ACT = mybir.ActivationFunctionType
AX = mybir.AxisListType

P = 128
BATCH, SEQ, DM = 4, 1024, 256
T = 512
TT = T // P
HALVES = SEQ // T
CHUNKS = BATCH * HALVES
KM = DM // P
DI = 512
G = DI // P
NS = 16
TAPS = 4
PAD = TAPS - 1
NE = 32
EN = NE // NS
TOPK = 8
NI = 128
ROWS = 8
LN_EPS, SUM_EPS = 1e-5, 1e-9
BELOW_ALL = -3.3e38


def build_program(nc, io):
    with ExitStack() as ctx:
        def sb(name, shape, dt=F32):
            return ctx.enter_context(nc.sbuf_tensor(name, shape, dt))

        def bank(name):
            return ctx.enter_context(nc.psum_tensor(name, [P, T], F32))

        def sem(name):
            return ctx.enter_context(nc.semaphore(name))

        in_wT = sb("in_wT", [P, KM, 2 * DI])
        dt_fused = sb("dt_fused", [P, G, DI])
        bc_wT = sb("bc_wT", [P, G, 2 * NS])
        out_wT = sb("out_wT", [P, G, DM])
        shared_w = sb("shared_w", [P, 6 * NI])
        router_w = sb("router_w", [P, KM, NE])
        router_b = sb("router_b", [1, NE])
        ones_row = sb("ones_row", [1, P])
        down_b = sb("down_b", [2 * NE + 1, DM])
        conv_w = sb("conv_w", [P, G, TAPS])
        conv_b = sb("conv_b", [P, G])
        dt_b = sb("dt_b", [P, G])
        a_log = sb("a_log", [P, NS * G])
        a_exp = sb("a_exp", [P, NS * G])
        a_neg = sb("a_neg", [P, NS * G])
        skip_d = sb("skip_d", [P, G])
        half_d = sb("half_d", [P, G])
        gate_b = sb("gate_b", [P, NE + 1])
        half_gate_b = sb("half_gate_b", [P, NE + 1])
        up_b = sb("up_b", [P, NE + 1])
        ident = sb("ident", [P, P])
        pick_raw = sb("pick_raw", [ROWS, ROWS // 2, P])
        pick = sb("pick", [ROWS, ROWS // 2, P], F32R)
        minus_half = sb("minus_half", [P, TT])

        x_in = [sb(f"x_in{i}", [P, TT, DM]) for i in range(2)]
        stats = sb("stats", [P, TT, 6])
        mean_var = sb("mean_var", [P, TT, 2])
        var_eps = sb("var_eps", [P, TT])
        rstd = sb("rstd", [P, TT])
        xn = sb("xn", [P, TT, DM])
        xnT = sb("xnT", [P, KM, T])
        logits = sb("logits", [P, TT, NE])
        top = sb("top", [P, TT, TOPK])
        without_top = sb("without_top", [P, TT, NE])
        chosen = sb("chosen", [P, TT, NE])
        aff_e = sb("aff_e", [P, TT, NE])
        aff_d = sb("aff_d", [P, TT, NE])
        aff = sb("aff", [P, TT, NE])
        aff_top = sb("aff_top", [P, TT, NE])
        aff_sum = sb("aff_sum", [P, TT])
        aff_sum_eps = sb("aff_sum_eps", [P, TT])
        aff_inv = sb("aff_inv", [P, TT])
        weight = sb("weight", [P, TT, NE])
        weight_split = sb("weight_split", [P, TT, 2, NE], F32R)
        weight_rows = sb("weight_rows", [2 * NE + 1, T])
        bc_hi = sb("bc_hi", [2 * NS, T], F32R)
        bc_lo = sb("bc_lo", [2 * NS, T], F32R)
        x_pad = sb("x_pad", [P, G, PAD + T])
        z_tanh = sb("z_tanh", [P, G, T])
        z_gate = sb("z_gate", [P, G, T])
        conv = sb("conv", [P, G, T])
        conv_tanh = sb("conv_tanh", [P, G, T])
        xs2 = sb("xs2", [P, G, T])
        sp_e = sb("sp_e", [P, G, T])
        sp_ln = sb("sp_ln", [P, G, T])
        sp_relu = sb("sp_relu", [P, G, T])
        delta = sb("delta", [P, G, T])
        du2 = sb("du2", [P, G, T])
        shared_sig = sb("shared_sig", [P, T])
        shared_silu = sb("shared_silu", [P, T])
        shared_up = sb("shared_up", [P, T])
        yz = sp_ln
        o_sb = sb("o_sb", [P, KM, T])
        o_tok = sb("o_tok", [P, TT, DM])

        w_gu = [sb(f"w_gu{i}", [P, EN, 4 * NI]) for i in range(2)]
        w_dn = [sb(f"w_dn{i}", [P, EN, DM]) for i in range(2)]
        rows = [sb(f"rows{i}", [ROWS, T], F32R) for i in range(2)]
        row_b0 = sb("row_b0", [2, T], F32R)
        u_in = conv_tanh
        h = sb("h", [P, G, T])
        h_last = sb("h_last", [P, NS, G])
        h_first = sb("h_first", [P, G])
        hc = z_tanh
        y = sb("y", [P, G, T])
        sig = [sb(f"sig{i}", [P, T]) for i in range(EN)]
        silu = sb("silu", [P, T])
        act_up = sb("act_up", [P, T])
        hidden = [sb(f"hidden{i}", [P, T]) for i in range(EN)]

        p_gate = bank("p_gate")
        p_up = bank("p_up")
        p_out = [bank(f"p_out{i}") for i in range(KM)]
        p_bc = bank("p_bc")
        p_w = bank("p_w")
        p_decay = [bank(f"p_decay{i}") for i in range(2)]

        x_banks = [p_w, p_decay[0], p_decay[1], p_gate]
        z_banks = [p_up, p_bc, p_w, p_decay[0]]
        dt_banks = [p_w, p_decay[0], p_decay[1], p_gate]

        def conv_done(g):
            return (g // 2) * 2 * TAPS + 2 * (TAPS - 1) + g % 2 + 1

        row_store = [nc.dram_tensor(f"row_store{i}", [NS, ROWS, T], F32).ap() for i in range(HALVES)]

        s_setup = sem("s_setup")
        s_apart = sem("s_apart")
        s_x = [sem(f"s_x{i}") for i in range(2)]
        s_wgu = [sem(f"s_wgu{i}") for i in range(2)]
        s_wdn = [sem(f"s_wdn{i}") for i in range(2)]
        s_rows = [sem(f"s_rows{i}") for i in range(2)]
        s_row_b0 = sem("s_row_b0")
        s_bc_stored = sem("s_bc_stored")
        s_w_stored = sem("s_w_stored")
        s_out = sem("s_out")
        s_fused = sem("s_fused")
        s_fused_kept = sem("s_fused_kept")
        s_a_exp = sem("s_a_exp")
        s_const_dve = sem("s_const_dve")
        s_const_pool = sem("s_const_pool")
        names = """stats mean_var var_eps rstd xn xn_tr xnT p_logits logits top without_top chosen aff_e aff_d aff
            aff_top aff_sum aff_sum_eps aff_inv weight weight_hi weight_lo weight_tr weight_rows p_x x_pad halo p_z
            z_tanh z_gate conv conv_tanh xs2 p_bc_proj bc_hi bc_lo p_dt sp_abs sp_relu sp_e sp_ln sp_back sp_rest
            sp_sum delta du2 y_init h_zero sh_gate sh_up sh_tanh sh_sig sh_silu sh_up_done sh_hidden sh_down""".split()
        S = {n: sem("s_" + n) for n in names}
        s_b = sem("s_b")
        s_c = sem("s_c")
        s_gate = sem("s_gate")
        s_up = sem("s_up")
        s_wb = sem("s_wb")
        s_down = sem("s_down")
        s_decay = sem("s_decay")
        s_tanh = sem("s_tanh")
        s_sig = sem("s_sig")
        s_h_first = sem("s_h_first")
        s_u_in = sem("s_u_in")
        s_scan = sem("s_scan")
        s_hc = sem("s_hc")
        s_h_last = sem("s_h_last")
        s_silu = sem("s_silu")
        s_act_up = sem("s_act_up")
        s_hidden = sem("s_hidden")
        s_y = sem("s_y")
        s_yz = sem("s_yz")
        s_o_proj = sem("s_o_proj")
        s_o_sb = sem("s_o_sb")
        s_o_tr = sem("s_o_tr")
        s_o_tok = sem("s_o_tok")

        block = ctx.enter_context(nc.Block())

        setup_loads = [
            (in_wT[:, :, :], io["in_wT"]), (bc_wT[:, :, :], io["bc_wT"]), (out_wT[:, :, :], io["out_wT"]),
            (shared_w[:, :], io["shared_w"]), (router_w[:, :, :], io["router_w"]), (router_b[:, :], io["router_b"]),
            (down_b[0:NE, :], io["down_b"]), (down_b[NE:2 * NE, :], io["down_b"]),
            (down_b[2 * NE:2 * NE + 1, :], io["shared_down_b"]),
            (conv_w[:, :, :], io["conv_w"]), (conv_b[:, :], io["conv_b"]), (dt_b[:, :], io["dt_b"]),
            (a_log[:, :], io["a_log"]), (skip_d[:, :], io["skip_d"]), (gate_b[:, :], io["gate_b"]),
            (up_b[:, :], io["up_b"]), (ident[:, :], io["ident"]), (pick_raw[:, :, :], io["pick"]),
            (sp_e[:, :, :], io["x_w"]), (sp_ln[:, :, :], io["dt_wT"]),
        ]
        SETUP = 16 * len(setup_loads)

        ONE = 1
        counted = [*S.values(), *s_x, *s_wgu, *s_wdn, *s_rows, s_row_b0, s_bc_stored, s_w_stored, s_out, s_b, s_c,
                   s_gate, s_up, s_wb, s_down, s_decay, s_tanh, s_sig, s_h_first, s_u_in, s_scan, s_hc, s_h_last,
                   s_silu, s_act_up, s_hidden, s_y, s_yz, s_o_proj, s_o_sb, s_o_tr, s_o_tok]

        def apart(eng):
            eng.sem_inc(s_apart, 1)

        def chunks(eng, body):
            with eng.Fori(0, BATCH) as b:
                for half in range(HALVES):
                    body(b, half, b * HALVES + half)

        def steps(eng, c, body, first=0, last=NS // 2):
            apart(eng)
            with eng.Fori(first, last) as t:
                turn = c * (NS // 2) + t
                for k in range(2):
                    body(k, turn, turn * 2 + k, t * 2 + k)

        def x_tile(dram, b, half):
            return dram[bass.ds(b, 1), half * T:(half + 1) * T, :].rearrange("o (t p) d -> p (o t) d", p=P)

        @block.sync
        def _(sp):
            for dst, src in setup_loads:
                sp.dma_start(dst, src).then_inc(s_setup, 16)
            for s in counted:
                sp.sem_inc(s, ONE)
            sp.dma_start(x_in[0][:, :, :], x_tile(io["x"], 0, 0)).then_inc(s_x[0], 16)

            def load_experts(k, s):
                sp.dma_start(w_gu[k][:, :, :], io["w_gu"][bass.ds(s, 1)].rearrange("o p e n -> p (o e) n"))\
                  .then_inc(s_wgu[k], 16)
                sp.dma_start(w_dn[k][:, :, :], io["w_dn"][bass.ds(s, 1)].rearrange("o p e n -> p (o e) n"))\
                  .then_inc(s_wdn[k], 16)

            for k in range(2):
                load_experts(k, k)

            def chunk(b, half, c):
                store = row_store[half]

                def load_rows(k, s):
                    sp.dma_start(rows[k][:, :].bitcast(F32), store[bass.ds(s, 1)].rearrange("o r t -> (o r) t"))\
                      .then_inc(s_rows[k], 16)

                sp.wait_ge(s_o_tok, ONE + 2 * c)
                apart(sp)
                nxt = b if half == 0 else (b + 1) % BATCH
                sp.dma_start(x_in[1 - half][:, :, :], x_tile(io["x"], nxt, 1 - half)).then_inc(s_x[1 - half], 16)
                sp.wait_ge(s_rows[0], ONE + 16 * (NS // 2) * c)
                apart(sp)
                sp.wait_ge(s_rows[1], ONE + 16 * (NS // 2) * c)
                apart(sp)
                sp.wait_ge(s_row_b0, ONE + 16 * c)
                apart(sp)
                sp.wait_ge(S["bc_hi"], ONE + c + 1)
                sp.dma_start(store[:, 0, :], bc_hi[0:NS, :].bitcast(F32)).then_inc(s_bc_stored, 16)
                sp.dma_start(store[:, 2, :], bc_hi[NS:2 * NS, :].bitcast(F32)).then_inc(s_bc_stored, 16)
                sp.wait_ge(S["bc_lo"], ONE + c + 1)
                sp.dma_start(store[:, 1, :], bc_lo[0:NS, :].bitcast(F32)).then_inc(s_bc_stored, 16)
                sp.dma_start(store[:, 3, :], bc_lo[NS:2 * NS, :].bitcast(F32)).then_inc(s_bc_stored, 16)
                sp.wait_ge(s_bc_stored, ONE + 64 * (c + 1))
                sp.dma_start(row_b0[:, :].bitcast(F32), store[NS - 1, 0:2, :]).then_inc(s_row_b0, 16)
                sp.wait_ge(S["weight_rows"], ONE + c + 1)
                for part in range(2):
                    for e in range(EN):
                        sp.dma_start(store[:, 4 + 2 * e + part, :],
                                     weight_rows[part * NE + e * NS:part * NE + (e + 1) * NS, :])\
                          .then_inc(s_w_stored, 16)
                sp.wait_ge(s_w_stored, ONE + 64 * (c + 1))
                for k in range(2):
                    load_rows(k, k)

                def refill(k, n, s, with_rows=True):
                    sp.wait_ge(s_up, ONE + EN * (n + 1))
                    apart(sp)
                    sp.dma_start(w_gu[k][:, :, :], io["w_gu"][bass.ds(s, 1)].rearrange("o p e n -> p (o e) n"))\
                      .then_inc(s_wgu[k], 16)
                    if with_rows:
                        sp.wait_ge(s_b, ONE + n + 2 + c)
                        sp.wait_ge(s_wb, ONE + EN * (n + 1))
                        apart(sp)
                        load_rows(k, s)
                    sp.wait_ge(s_down, ONE + EN * (n + 1))
                    apart(sp)
                    sp.dma_start(w_dn[k][:, :, :], io["w_dn"][bass.ds(s, 1)].rearrange("o p e n -> p (o e) n"))\
                      .then_inc(s_wdn[k], 16)

                steps(sp, c, lambda k, turn, n, s: refill(k, n, s + 2), 0, NS // 2 - 1)
                for k in range(2):
                    refill(k, c * NS + NS - 2 + k, k, with_rows=False)
                sp.wait_ge(s_o_tok, ONE + 2 * (c + 1))
                apart(sp)
                sp.dma_start(x_tile(io["out"], b, half), o_tok[:, :, :]).then_inc(s_out, 16)

            chunks(sp, chunk)
            sp.wait_ge(s_out, ONE + 16 * CHUNKS)

        @block.gpsimd
        def _(pool):
            pool.memset(minus_half[:, :], -0.5).then_inc(s_const_pool, 1)
            pool.wait_ge(s_const_pool, 1)
            pool.memset(ones_row[:, :], 1.0).then_inc(s_const_pool, 1)
            pool.wait_ge(s_const_pool, 2)
            pool.memset(weight_rows[2 * NE:2 * NE + 1, :], 1.0).then_inc(s_const_pool, 1)
            pool.wait_ge(s_const_pool, 3)

            def chunk(b, half, c):
                pool.wait_ge(S["conv"], ONE + G * TAPS * c)
                apart(pool)
                if half == 0:
                    pool.memset(x_pad[:, :, 0:PAD], 0.0).then_inc(S["halo"], 1)
                else:
                    pool.tensor_copy(x_pad[:, :, 0:PAD], x_pad[:, :, T:T + PAD]).then_inc(S["halo"], 1)
                pool.wait_ge(S["mean_var"], ONE + TT * (c + 1))
                pool.wait_ge(S["rstd"], ONE + c)
                apart(pool)
                pool.tensor_scalar(var_eps[:, :], mean_var[:, :, 1], LN_EPS, None, ALU.add).then_inc(S["var_eps"], 1)
                pool.wait_ge(S["var_eps"], ONE + c + 1)
                pool.wait_ge(S["xn"], ONE + TT * c)
                pool.tensor_tensor(rstd[:, :], var_eps[:, :], minus_half[:, :], ALU.pow).then_inc(S["rstd"], 1)
                for g in range(G):
                    pool.wait_ge(S["sp_back"], ONE + G * c + g + 1)
                    pool.tensor_tensor(delta[:, g, :], sp_e[:, g, :], delta[:, g, :], ALU.subtract)\
                        .then_inc(S["sp_rest"], 1)
                pool.wait_ge(S["y_init"], ONE + G * (c + 1))

                def step(k, turn, n, s):
                    pool.wait_ge(s_hc, ONE + n + 1)
                    pool.wait_ge(s_y, ONE + n)
                    pool.tensor_tensor(y[:, :, :], y[:, :, :], hc[:, :, :], ALU.add).then_inc(s_y, 1)

                steps(pool, c, step)

            chunks(pool, chunk)

        @block.scalar
        def _(act):
            act.wait_ge(s_setup, SETUP)
            act.activation(a_exp[:, :], a_log[:, :], ACT.Exp).then_inc(s_a_exp, 1)

            def chunk(b, half, c):
                act.wait_ge(S["halo"], ONE + c + 1)
                for g in range(G):
                    act.wait_ge(S["p_x"], ONE + G * c + g + 1)
                    act.activation(x_pad[:, g, PAD:PAD + T], x_banks[g][:, :], ACT.Copy).then_inc(S["x_pad"], 1)
                act.wait_ge(S["z_gate"], ONE + G * c)
                act.wait_ge(s_y, ONE + NS * c)
                for g in range(G):
                    act.wait_ge(S["p_z"], ONE + G * c + g + 1)
                    act.activation(z_tanh[:, g, :], z_banks[g][:, :], ACT.Tanh, scale=0.5).then_inc(S["z_tanh"], 1)
                act.wait_ge(S["sh_gate"], ONE + c + 1)
                act.wait_ge(S["sh_silu"], ONE + c)
                act.activation(shared_sig[:, :], p_decay[1][:, :], ACT.Tanh, scale=0.5,
                               bias=half_gate_b[:, NE:NE + 1]).then_inc(S["sh_tanh"], 1)
                act.wait_ge(S["logits"], ONE + c + 1)
                act.wait_ge(S["aff_d"], ONE + c)
                act.activation(aff_e[:, :, :], logits[:, :, :], ACT.Exp, scale=-1.0).then_inc(S["aff_e"], 1)
                act.wait_ge(S["xs2"], ONE + G * c)
                act.wait_ge(s_scan, ONE + G * NS * c)
                for g in range(G):
                    act.wait_ge(S["conv"], ONE + G * TAPS * c + conv_done(g))
                    act.activation(conv_tanh[:, g, :], conv[:, g, :], ACT.Tanh, scale=0.5).then_inc(S["conv_tanh"], 1)
                act.wait_ge(S["weight_tr"], ONE + c + 1)
                act.wait_ge(s_w_stored, ONE + 64 * c)
                act.wait_ge(S["sh_down"], ONE + c)
                act.activation(weight_rows[0:2 * NE, :], p_up[0:2 * NE, :], ACT.Copy).then_inc(S["weight_rows"], 1)
                act.wait_ge(S["delta"], ONE + G * c)
                for g in range(G):
                    act.wait_ge(S["p_dt"], ONE + G * c + g + 1)
                    act.activation(sp_e[:, g, :], dt_banks[g][:, :], ACT.Abs, bias=dt_b[:, g:g + 1])\
                       .then_inc(S["sp_abs"], 1)
                    act.activation(sp_relu[:, g, :], dt_banks[g][:, :], ACT.Relu, bias=dt_b[:, g:g + 1])\
                       .then_inc(S["sp_relu"], 1)
                for g in range(G):
                    act.wait_ge(S["sp_abs"], ONE + G * c + g + 1)
                    act.activation(sp_e[:, g, :], sp_e[:, g, :], ACT.Exp, scale=-1.0).then_inc(S["sp_e"], 1)
                act.wait_ge(s_o_proj, ONE + KM * c)
                for g in range(G):
                    act.wait_ge(S["sp_e"], ONE + G * c + g + 1)
                    act.activation(sp_ln[:, g, :], sp_e[:, g, :], ACT.Ln, bias=1.0).then_inc(S["sp_ln"], 1)
                act.wait_ge(s_yz, ONE + G * c)
                act.wait_ge(S["xs2"], ONE + G * (c + 1))
                for g in range(G):
                    act.activation(y[:, g, :], xs2[:, g, :], ACT.Copy, scale=half_d[:, g:g + 1])\
                       .then_inc(S["y_init"], 1)
                act.wait_ge(S["sp_relu"], ONE + G * (c + 1))
                act.wait_ge(S["delta"], ONE + G * (c + 1))

                def step(k, turn, n, s):
                    def decay(g, scans):
                        act.wait_ge(s_scan, ONE + scans)
                        act.activation(p_decay[g % 2][:, :], delta[:, g, :], ACT.Exp,
                                       scale=a_neg[:, bass.ds(s * G + g, 1)]).then_inc(s_decay, 1)

                    def gate_tanh(j):
                        act.wait_ge(s_gate, ONE + EN * n + j + 1)
                        act.wait_ge(s_silu, ONE + EN * n)
                        act.activation(sig[j][:, :], p_gate[:, :], ACT.Tanh, scale=0.5,
                                       bias=half_gate_b[:, bass.ds(s * EN + j, 1)]).then_inc(s_tanh, 1)

                    def gate_sig(j):
                        act.wait_ge(s_tanh, ONE + EN * n + j + 1)
                        act.activation(sig[j][:, :], sig[j][:, :], ACT.Identity, bias=1.0).then_inc(s_sig, 1)

                    decay(0, G * n)
                    decay(1, G * n)
                    gate_tanh(0)
                    decay(2, G * n + 1)
                    gate_sig(0)
                    decay(3, G * n + 2)
                    gate_tanh(1)
                    gate_sig(1)

                steps(act, c, step)
                act.wait_ge(s_o_tr, ONE + 2 * c)
                for m in range(KM):
                    act.wait_ge(s_o_proj, ONE + KM * c + m + 1)
                    act.activation(o_sb[:, m, :], p_out[m][:, :], ACT.Copy).then_inc(s_o_sb, 1)

            chunks(act, chunk)

        @block.vector
        def _(dve):
            dve.wait_ge(s_setup, SETUP)
            consts = [
                dve.tensor_copy(pick[:, :, :], pick_raw[:, :, :]),
                dve.tensor_scalar(half_gate_b[:, :], gate_b[:, :], 0.5, None, ALU.mult),
                dve.tensor_scalar(half_d[:, :], skip_d[:, :], 0.5, None, ALU.mult),
                dve.tensor_scalar(bc_wT[:, :, 0:NS], bc_wT[:, :, 0:NS], 0.25, None, ALU.mult),
                dve.tensor_scalar(bc_wT[:, :, NS:2 * NS], bc_wT[:, :, NS:2 * NS], 0.5, None, ALU.mult),
            ]
            for made in consts:
                made.then_inc(s_const_dve, 1)
            dve.wait_ge(s_a_exp, 1)
            dve.tensor_scalar(a_neg[:, :], a_exp[:, :], -1.0, None, ALU.mult).then_inc(s_const_dve, 1)
            for g in range(G):
                dve.wait_ge(s_fused, g + 1)
                dve.tensor_scalar(dt_fused[:, g, :], x_banks[g][:, :], 0.5, None, ALU.mult).then_inc(s_fused_kept, 1)

            def chunk(b, half, c):
                def done(name, per_chunk, made):
                    dve.wait_ge(S[name], ONE + per_chunk * c + made)

                dve.wait_ge(s_x[half], ONE + 16 * (b + 1))
                done("mean_var", TT, 0)
                for t in range(TT):
                    dve.bn_stats(stats[:, t, :], x_in[half][:, t, :]).then_inc(S["stats"], 1)
                dve.wait_ge(S["var_eps"], ONE + c)
                done("xn", TT, 0)
                for t in range(TT):
                    done("stats", TT, t + 1)
                    apart(dve)
                    dve.bn_aggr(mean_var[:, t, :], stats[:, t, :]).then_inc(S["mean_var"], 1)
                dve.wait_ge(S["rstd"], ONE + c + 1)
                dve.wait_ge(S["xn_tr"], ONE + KM * c)
                done("mean_var", TT, TT)
                for t in range(TT):
                    dve.tensor_scalar(xn[:, t, :], x_in[half][:, t, :], mean_var[:, t, 0:1], rstd[:, t:t + 1],
                                      ALU.subtract, ALU.mult).then_inc(S["xn"], 1)
                dve.wait_ge(s_up, ONE + NE * c)
                for k in range(KM):
                    dve.wait_ge(S["xn_tr"], ONE + KM * c + k + 1)
                    dve.tensor_copy(xnT[:, k, :], (p_gate, p_up)[k][:, :]).then_inc(S["xnT"], 1)
                dve.wait_ge(S["p_logits"], ONE + c + 1)
                done("aff_e", 1, 0)
                done("chosen", 1, 0)
                dve.tensor_copy(logits[:, :, :], p_bc[:, 0:TT * NE].rearrange("p (t e) -> p t e", e=NE))\
                   .then_inc(S["logits"], 1)

                dve.wait_ge(S["conv_tanh"], ONE + G * c)
                done("xs2", G, 0)
                for pair in range(G // 2):
                    for tap in range(TAPS):
                        for g in (2 * pair, 2 * pair + 1):
                            window = x_pad[:, g, tap:tap + T]
                            if tap == 0:
                                dve.wait_ge(S["x_pad"], ONE + G * c + g + 1)
                                dve.tensor_scalar(conv[:, g, :], window, conv_w[:, g, 0:1], conv_b[:, g:g + 1],
                                                  ALU.mult, ALU.add).then_inc(S["conv"], 1)
                            else:
                                done("conv", G * TAPS, (pair * TAPS + tap - 1) * 2 + g % 2 + 1)
                                dve.scalar_tensor_tensor(out=conv[:, g, :], in0=window,
                                                         scalar=conv_w[:, g, tap:tap + 1], in1=conv[:, g, :],
                                                         op0=ALU.mult, op1=ALU.add).then_inc(S["conv"], 1)
                dve.wait_ge(s_yz, ONE + G * c)
                for g in range(G):
                    dve.wait_ge(S["z_tanh"], ONE + G * c + g + 1)
                    dve.scalar_tensor_tensor(out=z_gate[:, g, :], in0=z_tanh[:, g, :], scalar=1.0,
                                             in1=z_banks[g][:, :], op0=ALU.add, op1=ALU.mult)\
                       .then_inc(S["z_gate"], 1)
                dve.wait_ge(S["sh_tanh"], ONE + c + 1)
                dve.tensor_scalar(shared_sig[:, :], shared_sig[:, :], 0.5, 0.5, ALU.mult, ALU.add)\
                   .then_inc(S["sh_sig"], 1)
                dve.wait_ge(S["y_init"], ONE + G * c)
                done("du2", G, 0)
                dve.wait_ge(S["p_dt"], ONE + G * c)
                for g in range(G):
                    dve.wait_ge(S["conv_tanh"], ONE + G * c + g + 1)
                    dve.scalar_tensor_tensor(out=xs2[:, g, :], in0=conv_tanh[:, g, :], scalar=1.0,
                                             in1=conv[:, g, :], op0=ALU.add, op1=ALU.mult).then_inc(S["xs2"], 1)
                done("sh_sig", 1, 1)
                done("sh_hidden", 1, 0)
                dve.scalar_tensor_tensor(out=shared_silu[:, :], in0=p_decay[1][:, :], scalar=gate_b[:, NE:NE + 1],
                                         in1=shared_sig[:, :], op0=ALU.add, op1=ALU.mult).then_inc(S["sh_silu"], 1)
                dve.wait_ge(S["sh_up"], ONE + c + 1)
                done("sh_silu", 1, 1)
                dve.wait_ge(S["sh_down"], ONE + c)
                dve.scalar_tensor_tensor(out=shared_up[:, :], in0=p_gate[:, :], scalar=up_b[:, NE:NE + 1],
                                         in1=shared_silu[:, :], op0=ALU.add, op1=ALU.mult)\
                   .then_inc(S["sh_hidden"], 1)
                dve.wait_ge(S["p_bc_proj"], ONE + c + 1)
                dve.wait_ge(s_bc_stored, ONE + 64 * c)
                dve.tensor_copy(bc_hi[:, :], p_bc[0:2 * NS, :]).then_inc(S["bc_hi"], 1)
                done("bc_hi", 1, 1)
                dve.tensor_tensor(bc_lo[:, :], p_bc[0:2 * NS, :], bc_hi[:, :].bitcast(F32), ALU.subtract)\
                   .then_inc(S["bc_lo"], 1)

                done("logits", 1, 1)
                done("without_top", TT, 0)
                apart(dve)
                for t in range(TT):
                    dve.max(top[:, t, :], logits[:, t, :]).then_inc(S["top"], 1)
                for t in range(TT):
                    done("top", TT, t + 1)
                    apart(dve)
                    dve.match_replace(without_top[:, t, :], in_to_replace=top[:, t, :], in_values=logits[:, t, :],
                                      imm_value=BELOW_ALL).then_inc(S["without_top"], 1)
                dve.wait_ge(S["aff_e"], ONE + c + 1)
                done("aff", 1, 0)
                dve.tensor_scalar(aff_d[:, :, :], aff_e[:, :, :], 1.0, None, ALU.add).then_inc(S["aff_d"], 1)
                done("without_top", TT, TT)
                done("aff_top", 1, 0)
                dve.tensor_tensor(chosen[:, :, :], without_top[:, :, :], logits[:, :, :], ALU.not_equal)\
                   .then_inc(S["chosen"], 1)
                done("aff_d", 1, 1)
                dve.reciprocal(aff[:, :, :], aff_d[:, :, :]).then_inc(S["aff"], 1)
                done("aff", 1, 1)
                done("chosen", 1, 1)
                done("weight", 1, 0)
                dve.tensor_tensor(aff_top[:, :, :], aff[:, :, :], chosen[:, :, :], ALU.mult).then_inc(S["aff_top"], 1)
                done("aff_top", 1, 1)
                dve.tensor_reduce(aff_sum[:, :], aff_top[:, :, :], AX.X, ALU.add).then_inc(S["aff_sum"], 1)
                done("aff_sum", 1, 1)
                dve.tensor_scalar(aff_sum_eps[:, :], aff_sum[:, :], SUM_EPS, None, ALU.add)\
                   .then_inc(S["aff_sum_eps"], 1)
                done("aff_sum_eps", 1, 1)
                dve.reciprocal(aff_inv[:, :], aff_sum_eps[:, :]).then_inc(S["aff_inv"], 1)
                done("aff_inv", 1, 1)
                done("weight_lo", 1, 0)
                dve.tensor_tensor(weight[:, :, :], aff_top[:, :, :],
                                  aff_inv[:, :].rearrange("p (t o) -> p t o", o=1).broadcast_to([P, TT, NE]),
                                  ALU.mult).then_inc(S["weight"], 1)
                done("weight", 1, 1)
                dve.wait_ge(S["weight_tr"], ONE + c)
                dve.tensor_copy(weight_split[:, :, 0, :], weight[:, :, :]).then_inc(S["weight_hi"], 1)
                done("weight_hi", 1, 1)
                dve.tensor_tensor(weight_split[:, :, 1, :], weight[:, :, :], weight_split[:, :, 0, :].bitcast(F32),
                                  ALU.subtract).then_inc(S["weight_lo"], 1)

                dve.wait_ge(s_decay, ONE + G * NS * c)
                done("xs2", G, G)
                dve.wait_ge(s_u_in, ONE + NS * c)
                for g in range(G):
                    dve.wait_ge(S["sp_e"], ONE + G * c + g + 1)
                    dve.tensor_scalar(delta[:, g, :], sp_e[:, g, :], 1.0, 1.0, ALU.add, ALU.subtract)\
                       .then_inc(S["sp_back"], 1)
                for g in range(G):
                    dve.wait_ge(S["sp_ln"], ONE + G * c + g + 1)
                    dve.wait_ge(S["sp_relu"], ONE + G * c + g + 1)
                    dve.tensor_tensor(sp_relu[:, g, :], sp_relu[:, g, :], sp_ln[:, g, :], ALU.add)\
                       .then_inc(S["sp_sum"], 1)
                for g in range(G):
                    dve.wait_ge(S["sp_rest"], ONE + G * c + g + 1)
                    done("sp_sum", G, g + 1)
                    dve.tensor_tensor(delta[:, g, :], sp_relu[:, g, :], delta[:, g, :], ALU.add)\
                       .then_inc(S["delta"], 1)
                for g in range(G):
                    done("delta", G, g + 1)
                    dve.tensor_tensor(du2[:, g, :], delta[:, g, :], xs2[:, g, :], ALU.mult).then_inc(S["du2"], 1)
                done("du2", G, G)
                if half == 0:
                    dve.wait_ge(s_h_last, ONE + NS * c)
                    dve.memset(h_last[:, :, :], 0.0).then_inc(S["h_zero"], 1)
                dve.wait_ge(S["h_zero"], ONE + b + 1)

                def step(k, turn, n, s):
                    def all_blocks(psum):
                        return psum[:, :].rearrange("p (o t) -> p o t", o=1).broadcast_to([P, G, T])

                    def scan(g):
                        dve.wait_ge(s_decay, ONE + G * n + g + 1)
                        dve.tensor_tensor_scan(h[:, g, :], p_decay[g % 2][:, :], u_in[:, g, :], h_first[:, g:g + 1],
                                               ALU.mult, ALU.add).then_inc(s_scan, 1)

                    def gated(j):
                        dve.wait_ge(s_sig, ONE + EN * n + j + 1)
                        dve.wait_ge(s_act_up, ONE + EN * n + j)
                        dve.scalar_tensor_tensor(out=silu[:, :], in0=p_gate[:, :],
                                                 scalar=gate_b[:, bass.ds(s * EN + j, 1)], in1=sig[j][:, :],
                                                 op0=ALU.add, op1=ALU.mult).then_inc(s_silu, 1)

                    def times_up(j):
                        dve.wait_ge(s_up, ONE + EN * n + j + 1)
                        dve.wait_ge(s_silu, ONE + EN * n + j + 1)
                        dve.wait_ge(s_hidden, ONE + EN * n + j)
                        dve.scalar_tensor_tensor(out=act_up[:, :], in0=p_up[:, :],
                                                 scalar=up_b[:, bass.ds(s * EN + j, 1)], in1=silu[:, :],
                                                 op0=ALU.add, op1=ALU.mult).then_inc(s_act_up, 1)

                    def times_weight(j):
                        dve.wait_ge(s_down, ONE + EN * n)
                        dve.wait_ge(s_wb, ONE + EN * n + j + 1)
                        dve.wait_ge(s_act_up, ONE + EN * n + j + 1)
                        dve.scalar_tensor_tensor(out=hidden[j][:, :], in0=act_up[:, :], scalar=0.5, in1=p_w[:, :],
                                                 op0=ALU.mult, op1=ALU.mult).then_inc(s_hidden, 1)

                    dve.wait_ge(s_h_last, ONE + n)
                    dve.wait_ge(s_scan, ONE + G * n)
                    dve.tensor_copy(h_first[:, :], h_last[:, bass.ds(s, 1), :].rearrange("p o g -> p (o g)"))\
                       .then_inc(s_h_first, 1)
                    dve.wait_ge(s_b, ONE + n + c + 1)
                    dve.tensor_tensor(u_in[:, :, :], du2[:, :, :], all_blocks(p_bc), ALU.mult).then_inc(s_u_in, 1)
                    dve.wait_ge(s_u_in, ONE + n + 1)
                    dve.wait_ge(s_h_first, ONE + n + 1)
                    dve.wait_ge(s_hc, ONE + n)
                    scan(0)
                    scan(1)
                    gated(0)
                    scan(2)
                    times_up(0)
                    scan(3)
                    times_weight(0)
                    dve.wait_ge(s_scan, ONE + G * (n + 1))
                    dve.wait_ge(s_c, ONE + n + 1)
                    dve.wait_ge(s_y, ONE + n)
                    dve.tensor_tensor(hc[:, :, :], h[:, :, :], all_blocks(p_bc), ALU.mult).then_inc(s_hc, 1)
                    dve.tensor_copy(h_last[:, bass.ds(s, 1), :].rearrange("p o g -> p (o g)"), h[:, :, T - 1])\
                       .then_inc(s_h_last, 1)
                    gated(1)
                    times_up(1)
                    times_weight(1)

                steps(dve, c, step)
                dve.wait_ge(s_y, ONE + NS * (c + 1))
                done("sp_sum", G, G)
                for g in range(G):
                    dve.scalar_tensor_tensor(out=yz[:, g, :], in0=y[:, g, :], scalar=0.5, in1=z_gate[:, g, :],
                                             op0=ALU.mult, op1=ALU.mult).then_inc(s_yz, 1)
                dve.wait_ge(s_out, ONE + 16 * c)
                for q in range(2):
                    dve.wait_ge(s_o_tr, ONE + 2 * c + q + 1)
                    dve.tensor_tensor(o_tok[:, 2 * q:2 * q + 2, :],
                                      p_decay[q][:, :].rearrange("p (t d) -> p t d", d=DM),
                                      x_in[half][:, 2 * q:2 * q + 2, :], ALU.add).then_inc(s_o_tok, 1)

            chunks(dve, chunk)

        @block.tensor
        def _(pe):
            pe.wait_ge(s_setup, SETUP)
            for g in range(G):
                for j in range(G):
                    mm = pe.matmul(x_banks[g][:, :], sp_e[:, j, g * P:(g + 1) * P], sp_ln[:, j, :],
                                   start=(j == 0), stop=(j == G - 1))
                mm.then_inc(s_fused, 1)
            pe.wait_ge(s_const_dve, 6)
            pe.wait_ge(s_const_pool, 3)
            pe.wait_ge(s_fused_kept, G)

            def chunk(b, half, c):
                pe.wait_ge(s_silu, ONE + NE * c)
                pe.wait_ge(s_act_up, ONE + NE * c)
                for k in range(KM):
                    for t in range(TT):
                        pe.wait_ge(S["xn"], ONE + TT * c + t + 1)
                        mm = pe.transpose((p_gate, p_up)[k][:, t * P:(t + 1) * P], xn[:, t, k * P:(k + 1) * P],
                                          ident[:, :])
                    mm.then_inc(S["xn_tr"], 1)
                pe.wait_ge(S["xnT"], ONE + KM * (c + 1))
                pe.wait_ge(s_hc, ONE + NS * c)
                for t in range(TT):
                    out = p_bc[:, t * NE:(t + 1) * NE]
                    for k in range(KM):
                        pe.matmul(out, xnT[:, k, t * P:(t + 1) * P], router_w[:, k, :], start=(k == 0), stop=False)
                    mm = pe.matmul(out, ones_row[:, :], router_b[:, :], start=False, stop=True)
                mm.then_inc(S["p_logits"], 1)

                def in_proj(m, out):
                    for k in range(KM):
                        mm = pe.matmul(out[:, :], in_wT[:, k, m * P:(m + 1) * P], xnT[:, k, :],
                                       start=(k == 0), stop=(k == KM - 1))
                    return mm

                pe.wait_ge(s_hidden, ONE + NE * c)
                pe.wait_ge(s_scan, ONE + G * NS * c)
                pe.wait_ge(s_o_tok, ONE + 2 * c)
                for g in range(G):
                    in_proj(g, x_banks[g]).then_inc(S["p_x"], 1)
                z_free = [(S["xnT"], KM * (c + 1)), (S["logits"], c + 1),
                          (S["x_pad"], G * c + 1), (S["x_pad"], G * c + 2)]
                for g in range(G):
                    pe.wait_ge(z_free[g][0], ONE + z_free[g][1])
                    in_proj(G + g, z_banks[g]).then_inc(S["p_z"], 1)
                for i, (out, s_made) in enumerate(((p_decay[1], S["sh_gate"]), (p_gate, S["sh_up"]))):
                    pe.wait_ge(S["x_pad"], ONE + G * c + 3 + i)
                    for k in range(KM):
                        mm = pe.matmul(out[:, :], shared_w[:, (2 * i + k) * NI:(2 * i + k + 1) * NI], xnT[:, k, :],
                                       start=(k == 0), stop=(k == KM - 1))
                    mm.then_inc(s_made, 1)
                pe.wait_ge(S["z_gate"], ONE + G * c + 2)
                for g in range(G):
                    pe.wait_ge(S["xs2"], ONE + G * c + g + 1)
                    mm = pe.matmul(p_bc[0:2 * NS, :], bc_wT[:, g, :], xs2[:, g, :], start=(g == 0), stop=(g == G - 1))
                mm.then_inc(S["p_bc_proj"], 1)
                dt_free = [(S["z_gate"], G * c + 3), (S["z_gate"], G * c + 4), (S["sh_silu"], c + 1),
                           (S["sh_hidden"], c + 1)]
                for m in range(G):
                    pe.wait_ge(dt_free[m][0], ONE + dt_free[m][1])
                    for g in range(G):
                        mm = pe.matmul(dt_banks[m][:, :], dt_fused[:, g, m * P:(m + 1) * P], xs2[:, g, :],
                                       start=(g == 0), stop=(g == G - 1))
                    mm.then_inc(S["p_dt"], 1)
                pe.wait_ge(S["z_gate"], ONE + G * c + 1)
                pe.wait_ge(S["weight_lo"], ONE + c + 1)
                apart(pe)
                for t in range(TT):
                    mm = pe.transpose(p_up[0:2 * NE, t * P:(t + 1) * P],
                                      weight_split[:, t, :, :].bitcast(F32).rearrange("p a e -> p (a e)"),
                                      ident[:, :])
                mm.then_inc(S["weight_tr"], 1)
                pe.wait_ge(s_o_sb, ONE + KM * c)
                pe.wait_ge(S["sh_hidden"], ONE + c + 1)
                pe.wait_ge(S["weight_rows"], ONE + c + 1)
                for m in range(KM):
                    pe.matmul(p_out[m][:, :], shared_w[:, 4 * NI + m * P:4 * NI + (m + 1) * P], shared_up[:, :],
                              start=True, stop=False)
                    mm = pe.matmul(p_out[m][:, :], down_b[:, m * P:(m + 1) * P], weight_rows[:, :],
                                   start=False, stop=False)
                mm.then_inc(S["sh_down"], 1)
                pe.wait_ge(s_row_b0, ONE + 16 * (c + 1))
                pe.wait_ge(S["bc_lo"], ONE + c + 1)
                pe.matmul(p_bc[:, :], pick[0:2, 0, :], row_b0[:, :], start=True, stop=True).then_inc(s_b, 1)
                pe.wait_ge(S["sp_relu"], ONE + G * (c + 1))

                def step(k, turn, n, s):
                    def gate(j):
                        pe.wait_ge(s_silu, ONE + EN * n + j)
                        for kk in range(KM):
                            mm = pe.matmul(p_gate[:, :], w_gu[k][:, j, kk * NI:(kk + 1) * NI], xnT[:, kk, :],
                                           start=(kk == 0), stop=(kk == KM - 1))
                        mm.then_inc(s_gate, 1)

                    def up(j):
                        pe.wait_ge(s_act_up, ONE + EN * n + j)
                        for kk in range(KM):
                            mm = pe.matmul(p_up[:, :], w_gu[k][:, j, (KM + kk) * NI:(KM + kk + 1) * NI],
                                           xnT[:, kk, :], start=(kk == 0), stop=(kk == KM - 1))
                        mm.then_inc(s_up, 1)

                    def spread_weight(j):
                        pe.wait_ge(s_hidden, ONE + EN * n + j)
                        pe.matmul(p_w[:, :], pick[:, 2 + j, :], rows[k][:, :], start=True, stop=True)\
                          .then_inc(s_wb, 1)

                    def down(j):
                        pe.wait_ge(s_hidden, ONE + EN * n + j + 1)
                        for m in range(KM):
                            mm = pe.matmul(p_out[m][:, :], w_dn[k][:, j, m * P:(m + 1) * P], hidden[j][:, :],
                                           start=False, stop=False)
                        mm.then_inc(s_down, 1)

                    pe.wait_ge(s_wgu[k], ONE + 16 * (turn + 1))
                    gate(0)
                    up(0)
                    pe.wait_ge(s_rows[k], ONE + 16 * (turn + 1))
                    pe.wait_ge(s_u_in, ONE + n + 1)
                    pe.matmul(p_bc[:, :], pick[:, 1, :], rows[k][:, :], start=True, stop=True).then_inc(s_c, 1)
                    spread_weight(0)
                    gate(1)
                    up(1)
                    spread_weight(1)
                    pe.wait_ge(s_wdn[k], ONE + 16 * (turn + 1))
                    down(0)
                    pe.wait_ge(s_hc, ONE + n + 1)
                    pe.matmul(p_bc[:, :], pick[:, 0, :], rows[k][:, :], start=True, stop=True).then_inc(s_b, 1)
                    down(1)

                steps(pe, c, step)
                for g in range(G):
                    pe.wait_ge(s_yz, ONE + G * c + g + 1)
                    for m in range(KM):
                        mm = pe.matmul(p_out[m][:, :], out_wT[:, g, m * P:(m + 1) * P], yz[:, g, :],
                                       start=False, stop=(g == G - 1))
                        if g == G - 1:
                            mm.then_inc(s_o_proj, 1)
                pe.wait_ge(s_o_sb, ONE + KM * (c + 1))
                pe.wait_ge(s_scan, ONE + G * NS * (c + 1))
                for q in range(2):
                    for t in range(2):
                        for m in range(KM):
                            mm = pe.transpose(p_decay[q][:, t * DM + m * P:t * DM + (m + 1) * P],
                                              o_sb[:, m, (2 * q + t) * P:(2 * q + t + 1) * P], ident[:, :])
                    mm.then_inc(s_o_tr, 1)

            chunks(pe, chunk)


def kernel(**inputs):
    import numpy as np
    import concourse.bacc as bacc
    from concourse.bass_utils import run_bass_kernel_spmd

    a = {k.split("_", 2)[2]: np.asarray(v) for k, v in inputs.items()}

    def blocks(w):
        return w.reshape(w.shape[0] // P, P, -1).transpose(1, 0, 2)

    def columns(v):
        return v.reshape(-1, P).T

    def expert(gate, up, down):
        lead = gate.shape[:-2]
        parts = [w.reshape(*lead, KM, P, NI)[..., k, :, :] for w in (gate, up) for k in range(KM)]
        return np.concatenate(parts, axis=-1), down

    x_proj = a["x_proj_w"]
    turned = np.roll(np.arange(NS), -1)
    bc = np.concatenate([x_proj[DI:DI + NS][turned], x_proj[DI + NS:]], axis=0)
    gu, dn = expert(a["Wg"], a["Wu"], a["Wd"])
    pairs = np.arange(NE).reshape(EN, NS).T
    gu_s, dn_s = expert(a["Wg_s"], a["Wu_s"], a["Wd_s"])
    order = pairs.reshape(-1)
    arrays = {
        "x": a["x"],
        "in_wT": blocks(a["in_proj_w"].T), "bc_wT": blocks(bc.T), "out_wT": blocks(a["out_proj_w"].T),
        "x_w": blocks(x_proj[:DI]), "dt_wT": blocks(a["dt_proj_w"].T),
        "shared_w": np.concatenate([gu_s, dn_s], axis=-1),
        "router_w": blocks(a["Wr"]), "router_b": a["br"].reshape(1, NE),
        "down_b": a["bd"], "shared_down_b": a["bd_s"].reshape(1, DM),
        "conv_w": blocks(a["conv_w"].reshape(DI, TAPS)), "conv_b": columns(a["conv_b"]),
        "dt_b": columns(a["dt_proj_b"]), "skip_d": columns(a["D"]),
        "a_log": blocks(a["A_log"]).transpose(0, 2, 1).reshape(P, NS * G),
        "gate_b": np.concatenate([a["bg"][order], a["bg_s"].reshape(1, NI)]).T,
        "up_b": np.concatenate([a["bu"][order], a["bu_s"].reshape(1, NI)]).T,
        "w_gu": gu[pairs].transpose(0, 2, 1, 3), "w_dn": dn[pairs].transpose(0, 2, 1, 3),
        "ident": np.eye(P, dtype=np.float32),
        "pick": np.repeat(np.repeat(np.eye(ROWS // 2, dtype=np.float32), 2, axis=0)[:, :, None], P, axis=2),
    }
    nc = bacc.Bacc("TRN2", target_bir_lowering=False, num_devices=1)
    feed, io = {}, {}
    for name, v in arrays.items():
        v = np.ascontiguousarray(v)
        feed[f"in_{name}"] = v
        io[name] = nc.dram_tensor(f"in_{name}", v.shape, mybir.dt.from_np(v.dtype), kind="ExternalInput").ap()
    io["out"] = nc.dram_tensor("out_y", (BATCH, SEQ, DM), F32, kind="ExternalOutput").ap()
    build_program(nc, io)
    result = run_bass_kernel_spmd(nc, [feed], core_ids=[0])
    return result.results[0]["out_y"]
```

```python
from contextlib import ExitStack

import concourse.bass as bass
from concourse import mybir

F32 = mybir.dt.float32
F32R = mybir.dt.float32r
ALU = mybir.AluOpType
ACT = mybir.ActivationFunctionType
AX = mybir.AxisListType

P = 128
BATCH, SEQ, DM = 4, 1024, 256
T = 512
TT = T // P
HALVES = SEQ // T
CHUNKS = BATCH * HALVES
KM = DM // P
DI = 512
G = DI // P
NS = 16
TAPS = 4
PAD = TAPS - 1
NE = 32
EN = NE // NS
TOPK = 8
NI = 128
PARTS = 2
ROWS = 8
LN_EPS, SUM_EPS = 1e-5, 1e-9
BELOW_ALL = -3.3e38


def build_program(nc, io):
    with ExitStack() as ctx:
        def sb(name, shape, dt=F32):
            return ctx.enter_context(nc.sbuf_tensor(name, shape, dt))

        def bank(name):
            return ctx.enter_context(nc.psum_tensor(name, [P, T], F32))

        def sem(name):
            return ctx.enter_context(nc.semaphore(name))

        in_w = sb("in_w", [P, PARTS, KM, 2 * DI], F32R)
        dt_fused = sb("dt_fused", [P, G, DI])
        bc_wT = sb("bc_wT", [P, G, 2 * NS])
        out_wT = sb("out_wT", [P, G, DM])
        shared_gu = sb("shared_gu", [P, PARTS, 4 * NI], F32R)
        shared_dn = sb("shared_dn", [P, 2 * NI])
        router_w = sb("router_w", [P, KM, NE])
        router_b = sb("router_b", [1, NE])
        ones_row = sb("ones_row", [1, P])
        down_b = sb("down_b", [2 * NE, DM])
        shared_down_b = sb("shared_down_b", [P, KM])
        conv_w = sb("conv_w", [P, G, TAPS])
        conv_b = sb("conv_b", [P, G])
        dt_b = sb("dt_b", [P, G])
        a_neg = sb("a_neg", [P, NS * G])
        half_d = sb("half_d", [P, G])
        gate_b = sb("gate_b", [P, NE + 1])
        half_gate_b = sb("half_gate_b", [P, NE + 1])
        up_b = sb("up_b", [P, NE + 1])
        ident = sb("ident", [P, P])
        pick = sb("pick", [ROWS, ROWS // 2, P], F32R)
        minus_half = sb("minus_half", [P, TT])
        no_past = sb("no_past", [P, G, PAD])

        x_ln = sb("x_ln", [P, TT, DM])
        x_res = sb("x_res", [P, TT, DM])
        stats = sb("stats", [P, TT, 6])
        mean_var = sb("mean_var", [P, TT, 2])
        var_eps = sb("var_eps", [P, TT])
        rstd = sb("rstd", [P, TT])
        xnT = [sb(f"xnT{i}", [P, PARTS, KM, T], F32R) for i in range(2)]
        logits = sb("logits", [P, TT, NE])
        top = sb("top", [P, TT, TOPK])
        without_top = sb("without_top", [P, TT, NE])
        chosen = sb("chosen", [P, TT, NE])
        aff_e = sb("aff_e", [P, TT, NE])
        aff = sb("aff", [P, TT, NE])
        aff_top = sb("aff_top", [P, TT, NE])
        aff_sum = sb("aff_sum", [P, TT])
        aff_inv = sb("aff_inv", [P, TT])
        weight_split = sb("weight_split", [P, TT, 2, NE], F32R)
        weight_rows = x_res[0:2 * NE, TT // 2:TT, :].rearrange("p a d -> p (a d)")
        x_pad = [sb(f"x_pad{i}", [P, PAD + T]) for i in range(2)]
        bc_hi, bc_lo = (tile[0:2 * NS, 0:T].bitcast(F32R) for tile in x_pad)
        past = sb("past", [P, G, PAD])
        z_tanh = sb("z_tanh", [P, T])
        shared_sig = z_tanh
        z_gate = sb("z_gate", [P, G, T])
        scratch = sb("scratch", [P, G, T])
        conv = [scratch[:, i, :] for i in range(2)]
        conv_tanh = [scratch[:, 2 + i, :] for i in range(2)]
        sp_ln = scratch
        xs2 = sb("xs2", [P, G, T])
        sp_e = sb("sp_e", [P, G, T])
        delta = [sb(f"delta{i}", [P, G, T]) for i in range(2)]
        du2 = sb("du2", [P, G, T])
        shared_up = x_res[:, 0:TT // 2, :].rearrange("p a d -> p (a d)")
        o_area = sb("o_area", [P, G, T])
        o_sb = o_area[:, 0:KM, :]
        o_tok = o_area[:, KM:G, :].rearrange("p a (b d) -> p (a b) d", d=DM)
        sp_back = o_area

        w_gu = [sb(f"w_gu{i}", [P, PARTS, EN, 4 * NI], F32R) for i in range(2)]
        w_dn = [sb(f"w_dn{i}", [P, PARTS, EN, DM], F32R) for i in range(2)]
        rows = [sb(f"rows{i}", [ROWS, T], F32R) for i in range(2)]
        row_b0 = sb("row_b0", [2, T], F32R)
        h = sb("h", [P, G, T])
        u_in = h
        h_last = sb("h_last", [P, NS, G])
        hc = sb("hc", [P, G, T])
        y = sb("y", [P, G, T])
        act_tile = [sb(f"act_tile{i}", [P, T]) for i in range(EN)]
        gate_in = [sb(f"gate_in{i}", [P, T]) for i in range(EN)]
        hid_hi = [sb(f"hid_hi{i}", [P, T], F32R) for i in range(EN)]
        hid_lo = [sb(f"hid_lo{i}", [P, T], F32R) for i in range(EN)]
        pick_raw = y[0:ROWS, :, 0:P]
        a_exp = h[:, 0, 0:NS * G]
        a_log = h[:, 2, 0:NS * G]
        skip_d = h[:, 1, 0:G]
        x_w, dt_wT = sp_e, hc
        in_w_raw = scratch[:, :, :].rearrange("p (k a) t -> p k (a t)", k=KM)
        shared_gu_raw = xs2[:, 0, :]

        p_gate = bank("p_gate")
        p_up = bank("p_up")
        p_out = [bank(f"p_out{i}") for i in range(KM)]
        p_bc = bank("p_bc")
        p_w = bank("p_w")
        p_decay = bank("p_decay")
        p_side = bank("p_side")

        fused_banks = [p_gate, p_up, p_w, p_decay]

        row_store = [nc.dram_tensor(f"row_store{i}", [NS, ROWS, T], F32).ap() for i in range(HALVES)]
        gu_store = nc.dram_tensor("gu_store", [NS, P, PARTS, EN, 4 * NI], F32).ap()
        dn_store = nc.dram_tensor("dn_store", [NS, P, PARTS, EN, DM], F32).ap()

        s_setup = sem("s_setup")
        s_apart = sem("s_apart")
        s_fused = sem("s_fused")
        s_fused_kept = sem("s_fused_kept")
        s_a_exp = sem("s_a_exp")
        s_const_dve = sem("s_const_dve")
        s_const_pool = sem("s_const_pool")
        s_raw_gu = [sem(f"s_raw_gu{i}") for i in range(2)]
        s_raw_dn = [sem(f"s_raw_dn{i}") for i in range(2)]
        s_raw_copied = sem("s_raw_copied")
        s_w_hi = sem("s_w_hi")
        s_w_lo = sem("s_w_lo")
        s_kept = sem("s_kept")
        s_x_ln = sem("s_x_ln")
        s_x_res = sem("s_x_res")
        s_wgu = [sem(f"s_wgu{i}") for i in range(2)]
        s_wdn = [sem(f"s_wdn{i}") for i in range(2)]
        s_rows = [sem(f"s_rows{i}") for i in range(2)]
        s_row_b0 = sem("s_row_b0")
        s_bc_stored = sem("s_bc_stored")
        s_w_stored = sem("s_w_stored")
        s_out = sem("s_out")
        s_filled = sem("s_filled")
        s_read = sem("s_read")
        names = """xnT_hi stats mean_var var_eps rstd xn top without_top chosen aff_e aff_d aff aff_top aff_sum aff_sum_eps
            aff_inv weight weight_hi weight_lo past_in past_out conv conv_tanh xs2 bc_hi z_tanh sh_tanh sh_sig
            sh_down sp_abs sp_e sp_ln sp_back sp_rest sp_sum delta du2 y_init h_zero bias yz o_sb o_sum""".split()
        S = {n: sem("s_" + n) for n in names}
        s_b = sem("s_b")
        s_c = sem("s_c")
        s_gate = sem("s_gate")
        s_up = sem("s_up")
        s_wb = sem("s_wb")
        s_down = sem("s_down")
        s_decay = sem("s_decay")
        s_tanh = sem("s_tanh")
        s_sig = sem("s_sig")
        s_gate_in = sem("s_gate_in")
        s_u_in = sem("s_u_in")
        s_scan = sem("s_scan")
        s_hc = sem("s_hc")
        s_h_last = sem("s_h_last")
        s_silu = sem("s_silu")
        s_act_up = sem("s_act_up")
        s_hidden = sem("s_hidden")
        s_hid_hi = sem("s_hid_hi")
        s_hid_lo = sem("s_hid_lo")
        s_y = sem("s_y")

        block = ctx.enter_context(nc.Block())

        setup_loads = [
            (in_w_raw[:, :, :], io["in_wT"]), (bc_wT[:, :, :], io["bc_wT"]), (out_wT[:, :, :], io["out_wT"]),
            (shared_gu_raw, io["shared_w"][:, 0:4 * NI]),
            (shared_dn[:, :], io["shared_w"][:, 4 * NI:6 * NI]), (router_w[:, :, :], io["router_w"]), (router_b[:, :], io["router_b"]),
            (down_b[0:NE, :], io["down_b"]), (down_b[NE:2 * NE, :], io["down_b"]),
            (shared_down_b[:, :], io["shared_down_b"]),
            (conv_w[:, :, :], io["conv_w"]), (conv_b[:, :], io["conv_b"]), (dt_b[:, :], io["dt_b"]),
            (a_log, io["a_log"]), (skip_d, io["skip_d"]), (gate_b[:, :], io["gate_b"]),
            (up_b[:, :], io["up_b"]), (ident[:, :], io["ident"]), (pick_raw, io["pick"]),
            (x_w[:, :, :], io["x_w"]), (dt_wT[:, :, :], io["dt_wT"]),
        ]
        SETUP = 16 * len(setup_loads)

        ONE = 1
        counted = [*S.values(), s_x_ln, s_x_res, *s_wgu, *s_wdn, *s_rows, s_row_b0, s_bc_stored, s_w_stored, s_out,
                   s_filled, s_read, s_b, s_c, s_gate, s_up, s_wb, s_down, s_decay, s_tanh, s_sig, s_gate_in, s_u_in, s_scan,
                   s_hc, s_h_last, s_silu, s_act_up, s_hidden, s_hid_hi, s_hid_lo, s_y]

        FILLS = {
            (1, "A"): ("post", "out_proj0"), (2, "A"): ("post", "out_proj1"), (2, "B"): ("pre", "xnT0"),
            (3, "A"): ("pre", "xnT1"), (3, "B"): ("own", "z0"),
            (4, "A"): ("pre", "x0"), (4, "B"): ("pre", "logits"),
            (5, "A"): ("pre", "x1"), (5, "B"): ("post", "tokens0"),
            (6, "A"): ("pre", "x2"), (6, "B"): ("post", "tokens1"),
            (7, "A"): ("pre", "x3"), (7, "B"): ("own", "z1"),
            (8, "A"): ("own", "shared_gate"), (8, "B"): ("own", "shared_up"),
            (9, "A"): ("pre", "bc"), (9, "B"): ("own", "z2"),
            (10, "A"): ("pre", "dt0"), (11, "A"): ("pre", "dt1"), (12, "A"): ("pre", "dt2"), (12, "B"): ("own", "z3"),
            (13, "A"): ("pre", "dt3"), (13, "B"): ("pre", "weights"),
        }
        COUNT = {kind: sum(k == kind for k, _ in FILLS.values()) for kind in ("post", "pre", "own")}

        class Chunk:

            def __init__(self, c, b, half, post, own, pre, fills_before):
                self.c, self.b, self.half = c, b, half
                self.kinds = {k for k, on in (("post", post), ("own", own), ("pre", pre)) if on}
                self.fills_before = fills_before
                self.order = [name for kind, name in FILLS.values() if kind in self.kinds]

            def fill(self, name):
                return self.fills_before + self.order.index(name) + 1

            def next_place(self):
                return (self.b, 1) if self.half == 0 else (self.b + 1, 0)

            def last_place(self):
                return (self.b, 0) if self.half == 1 else (self.b - 1, 1)

        start = Chunk(-1, -1, 1, False, False, True, 0)
        ahead = COUNT["pre"]
        every = sum(COUNT.values())
        first_chunk = Chunk(0, 0, 0, False, True, True, ahead)
        ahead += COUNT["pre"] + COUNT["own"]

        def all_chunks(eng, sides, steps):
            sides(start)
            steps(first_chunk)
            apart(eng)
            with eng.Fori(0, BATCH - 1) as b:
                steps(Chunk(b * 2 + 1, b, 1, True, True, True, ahead + b * (2 * every)))
                steps(Chunk(b * 2 + 2, b + 1, 0, True, True, True, ahead + b * (2 * every) + every))
            n = CHUNKS - 1
            steps(Chunk(n, BATCH - 1, 1, True, True, False, ahead + (n - 1) * every))
            sides(Chunk(CHUNKS, BATCH, 0, True, False, False, ahead + n * every - COUNT["pre"]))

        def beside(table, ch, s, place):
            for kind, work in table.get((s, place), ()):
                if kind in ch.kinds:
                    work(ch)

        def alone(table):
            def run(ch):
                for s, place in sorted(table, key=lambda at: (at[0], PLACES.index(at[1]))):
                    beside(table, ch, s, place)
            return run

        PLACES = ["start", "early", "A", "B", "late"]

        def apart(eng):
            eng.sem_inc(s_apart, 1)

        def x_tile(dram, place):
            b, half = place
            return dram[bass.ds(b, 1), half * T:(half + 1) * T, :].rearrange("o (t p) d -> p (o t) d", p=P)

        @block.sync
        def _(sp):
            for dst, src in setup_loads:
                sp.dma_start(dst, src).then_inc(s_setup, 16)
            sp.dma_start(x_ln[:, :, :], x_tile(io["x"], (0, 0))).then_inc(s_x_ln, 16)
            for s in counted:
                sp.sem_inc(s, ONE)

            def load_gu(k, s):
                sp.dma_start(w_gu[k][:, :, :, :].bitcast(F32), gu_store[s]).then_inc(s_wgu[k], 16)

            def load_dn(k, s):
                sp.dma_start(w_dn[k][:, :, :, :].bitcast(F32), dn_store[s]).then_inc(s_wdn[k], 16)

            for at in range(0, NS, NS // 4):
                some = slice(at, at + NS // 4)
                sp.dma_start(gu_store[some, :, 1, :, :], io["w_gu"][some]).then_inc(s_raw_copied, 16)
                sp.dma_start(dn_store[some, :, 1, :, :], io["w_dn"][some]).then_inc(s_raw_copied, 16)

            def load_raw_gu(k, s):
                sp.dma_start(w_gu[k][:, 1, :, :].bitcast(F32), gu_store[s, :, 1, :, :]).then_inc(s_raw_gu[k], 16)

            def load_raw_dn(k, s):
                sp.dma_start(w_dn[k][:, 1, :, :].bitcast(F32), dn_store[s, :, 1, :, :]).then_inc(s_raw_dn[k], 16)

            def keep_split(s):
                sp.wait_ge(s_w_lo, s + 1)
                sp.dma_start(gu_store[s], w_gu[s % 2][:, :, :, :].bitcast(F32)).then_inc(s_kept, 16)
                sp.dma_start(dn_store[s], w_dn[s % 2][:, :, :, :].bitcast(F32)).then_inc(s_kept, 16)

            sp.wait_ge(s_raw_copied, 16 * 8)
            for k in range(2):
                load_raw_gu(k, k)
                load_raw_dn(k, k)

            def load_x_res(ch):
                own = "own" in ch.kinds
                for s_over, count in ((s_read, ch.fills_before), (S["sh_down"], ch.c), (S["bias"], ch.c + own),
                                      (s_w_stored, 64 * (ch.c + own))):
                    sp.wait_ge(s_over, ONE + count)
                    apart(sp)
                sp.dma_start(x_res[:, :, :], x_tile(io["x"], ch.last_place())).then_inc(s_x_res, 16)

            def load_next_x(ch):
                nxt = ((ch.b + 1) % BATCH, ch.half)
                sp.wait_ge(s_filled, ONE + ch.fill("xnT1"))
                apart(sp)
                sp.dma_start(x_ln[:, :, :], x_tile(io["x"], nxt)).then_inc(s_x_ln, 16)

            def store_bc(ch):
                _, half = ch.next_place()
                store = row_store[half]
                if ch is not start:
                    for s_loaded, loads in ((s_rows[0], NS // 2), (s_rows[1], NS // 2), (s_row_b0, 1)):
                        sp.wait_ge(s_loaded, ONE + 16 * loads * ch.c)
                        apart(sp)
                sp.wait_ge(S["bc_hi"], ONE + ch.c + 2)
                apart(sp)
                sp.dma_start(store[:, 0, :], bc_hi[0:NS, :].bitcast(F32)).then_inc(s_bc_stored, 16)
                sp.dma_start(store[:, 2, :], bc_hi[NS:2 * NS, :].bitcast(F32)).then_inc(s_bc_stored, 16)
                sp.wait_ge(s_read, ONE + ch.fill("bc"))
                apart(sp)
                sp.dma_start(store[:, 1, :], bc_lo[0:NS, :].bitcast(F32)).then_inc(s_bc_stored, 16)
                sp.dma_start(store[:, 3, :], bc_lo[NS:2 * NS, :].bitcast(F32)).then_inc(s_bc_stored, 16)

            def load_b0(ch):
                _, half = ch.next_place()
                sp.wait_ge(s_bc_stored, ONE + 64 * (ch.c + 2))
                apart(sp)
                if ch is not start:
                    sp.wait_ge(s_b, ONE + NS * ch.c + 1)
                    apart(sp)
                sp.dma_start(row_b0[:, :].bitcast(F32), row_store[half][NS - 1, 0:2]).then_inc(s_row_b0, 16)

            def store_weights(ch):
                _, half = ch.next_place()
                sp.wait_ge(s_read, ONE + ch.fill("weights"))
                apart(sp)
                for part in range(2):
                    for e in range(EN):
                        sp.dma_start(row_store[half][:, 4 + 2 * e + part, :],
                                     weight_rows[part * NE + e * NS:part * NE + (e + 1) * NS, :])\
                          .then_inc(s_w_stored, 16)

            def store_out(ch):
                sp.wait_ge(s_read, ONE + ch.fill("tokens1"))
                apart(sp)
                sp.dma_start(x_tile(io["out"], ch.last_place()), o_tok[:, :, :]).then_inc(s_out, 16)

            def first_rows(ch):
                _, half = ch.next_place()
                sp.wait_ge(s_w_stored, ONE + 64 * (ch.c + 2))
                sp.wait_ge(s_bc_stored, ONE + 64 * (ch.c + 2))
                apart(sp)

            table = {
                (0, "late"): [("post", load_x_res)],
                (4, "late"): [("pre", load_next_x)],
                (7, "early"): [("post", store_out)],
                (9, "late"): [("pre", store_bc)],
                (10, "late"): [("pre", load_b0)],
                (14, "A"): [("pre", store_weights)],
            }

            def sides(ch):
                if ch is start:
                    keep_split(0)
                    load_next_x(ch)
                    store_bc(ch)
                    load_b0(ch)
                    store_weights(ch)
                    first_rows(ch)
                    for s in range(2):
                        sp.dma_start(rows[s][:, :].bitcast(F32), row_store[0][s]).then_inc(s_rows[s], 16)
                else:
                    load_x_res(ch)
                    store_out(ch)

            def steps(ch):
                first = ch is first_chunk
                for s in range(NS):
                    n, k = ch.c * NS + s, s % 2
                    pre = "pre" in ch.kinds
                    beside(table, ch, s, "early")
                    if first:
                        sp.wait_ge(s_kept, 32 * (s + 1))
                    if (s + 1 < NS or pre) and not (first and s == 0):
                        sp.wait_ge(s_down, ONE + EN * n)
                        apart(sp)
                        (load_raw_dn if first and s + 1 < NS else load_dn)(1 - k, (s + 1) % NS)
                    if s + 2 < NS or pre:
                        sp.wait_ge(s_up, ONE + EN * (n + 1))
                        apart(sp)
                        (load_raw_gu if first and s + 2 < NS else load_gu)(k, (s + 2) % NS)
                    beside(table, ch, s, "A")
                    if s == NS - 2 and pre:
                        first_rows(ch)
                    if s + 2 < NS or pre:
                        sp.wait_ge(s_b, ONE + n + 2)
                        sp.wait_ge(s_wb, ONE + EN * (n + 1))
                        apart(sp)
                        store = row_store[ch.half if s + 2 < NS else ch.next_place()[1]]
                        sp.dma_start(rows[k][:, :].bitcast(F32), store[(s + 2) % NS]).then_inc(s_rows[k], 16)
                    if first and s + 1 < NS:
                        keep_split(s + 1)
                    beside(table, ch, s, "late")

            all_chunks(sp, sides, steps)
            sp.wait_ge(s_out, ONE + 16 * CHUNKS)

        @block.gpsimd
        def _(pool):
            pool.memset(minus_half[:, :], -0.5).then_inc(s_const_pool, 1)
            pool.wait_ge(s_const_pool, 1)
            pool.memset(ones_row[:, :], 1.0).then_inc(s_const_pool, 1)
            pool.wait_ge(s_const_pool, 2)
            pool.memset(no_past[:, :, :], 0.0).then_inc(s_const_pool, 1)
            pool.wait_ge(s_const_pool, 3)

            def make_rstd(ch):
                n = ch.c + 1
                pool.wait_ge(S["mean_var"], ONE + TT * (n + 1))
                pool.wait_ge(S["rstd"], ONE + n)
                apart(pool)
                pool.tensor_scalar(var_eps[:, :], mean_var[:, :, 1], LN_EPS, None, ALU.add).then_inc(S["var_eps"], 1)
                pool.wait_ge(S["var_eps"], ONE + n + 1)
                pool.wait_ge(S["xn"], ONE + TT * n)
                pool.tensor_tensor(rstd[:, :], var_eps[:, :], minus_half[:, :], ALU.pow).then_inc(S["rstd"], 1)

            def softplus_rest(ch):
                n = ch.c + 1
                pool.wait_ge(S["sp_back"], ONE + G * (n + 1))
                pool.tensor_tensor(sp_back[:, :, :], sp_e[:, :, :], sp_back[:, :, :], ALU.subtract)\
                    .then_inc(S["sp_rest"], 1)

            table = {
                (1, "late"): [("pre", make_rstd)],
                (14, "late"): [("pre", softplus_rest)],
            }

            def split_low(s):
                k = s % 2
                for tile in (w_gu[k], w_dn[k]):
                    pool.wait_ge(s_w_hi, s + 1)
                    made = pool.tensor_tensor(tile[:, 1, :, :], tile[:, 1, :, :].bitcast(F32),
                                              tile[:, 0, :, :].bitcast(F32), ALU.subtract)
                made.then_inc(s_w_lo, 1)

            def steps(ch):
                if ch is first_chunk:
                    split_low(0)
                for s in range(NS):
                    def add_y(n, part):
                        pool.wait_ge(s_hc, ONE + n + 1)
                        pool.wait_ge(s_y, ONE + 2 * n + part)
                        blocks = slice(2 * part, 2 * part + 2)
                        pool.tensor_tensor(y[:, blocks, :], y[:, blocks, :], hc[:, blocks, :], ALU.add)\
                            .then_inc(s_y, 1)

                    def silu(n, j):
                        pool.wait_ge(s_sig, ONE + EN * n + j + 1)
                        pool.tensor_tensor(act_tile[j][:, :], act_tile[j][:, :], gate_in[j][:, :], ALU.mult)\
                            .then_inc(s_silu, 1)

                    def low(n, j):
                        pool.wait_ge(s_hid_hi, ONE + EN * n + j + 1)
                        pool.tensor_tensor(hid_lo[j][:, :], act_tile[j][:, :], hid_hi[j][:, :].bitcast(F32), ALU.subtract)\
                            .then_inc(s_hid_lo, 1)

                    n = ch.c * NS + s
                    beside(table, ch, s, "early")
                    if s == 1:
                        pool.wait_ge(S["y_init"], ONE + G * (ch.c + 1))
                        apart(pool)
                    if s > 0:
                        add_y(n - 1, 0)
                        low(n - 1, 1)
                    silu(n, 0)
                    if s > 0:
                        add_y(n - 1, 1)
                    silu(n, 1)
                    low(n, 0)
                    if s == NS - 1:
                        low(n, 1)
                        add_y(n, 0)
                        add_y(n, 1)
                    if ch is first_chunk and s + 1 < NS:
                        split_low(s + 1)
                    beside(table, ch, s, "late")

            all_chunks(pool, alone(table), steps)

        @block.scalar
        def _(act):
            act.wait_ge(s_setup, SETUP)
            act.activation(a_exp, a_log, ACT.Exp).then_inc(s_a_exp, 1)

            def take_out(ch):
                act.wait_ge(s_down, ONE + NE * ch.c)
                act.wait_ge(S["sh_down"], ONE + ch.c)
                act.wait_ge(s_read, ONE + ch.fills_before)
                act.wait_ge(S["delta"], ONE + ch.c + ("own" in ch.kinds))
                for m in range(KM):
                    act.activation(o_sb[:, m, :], p_out[m][:, :], ACT.Identity,
                                   bias=shared_down_b[:, m:m + 1]).then_inc(S["o_sb"], 1)

            def y_init(ch):
                act.wait_ge(S["yz"], ONE + G * ch.c)
                for g in range(G):
                    act.activation(y[:, g, :], xs2[:, g, :], ACT.Copy, scale=half_d[:, g:g + 1])\
                       .then_inc(S["y_init"], 1)

            def take_xnT(k):
                def work(ch):
                    act.wait_ge(s_up, ONE + NE * ch.c if ch is not start else ONE)
                    act.wait_ge(s_filled, ONE + ch.fill(f"xnT{k}"))
                    act.activation(xnT[ch.next_place()[1]][:, 0, k, :], p_side[:, :], ACT.Copy).then_inc(S["xnT_hi"], 1)
                return work

            def take_x(g):
                def work(ch):
                    n, (_, half), tile = ch.c + 1, ch.next_place(), x_pad[g % 2]
                    act.wait_ge(s_bc_stored, ONE + 64 * n)
                    act.wait_ge(S["conv"], ONE + TAPS * (G * n + g - 1) if g > 1 else ONE + TAPS * G * n)
                    source = no_past if half == 0 else past
                    act.wait_ge(S["past_out"], ONE + G * n + g)
                    act.activation(tile[:, 0:PAD], source[:, g, :], ACT.Copy).then_inc(S["past_in"], 1)
                    act.wait_ge(s_filled, ONE + ch.fill(f"x{g}"))
                    act.activation(tile[:, PAD:PAD + T], p_side[:, :], ACT.Copy).then_inc(s_read, 1)
                    act.wait_ge(s_read, ONE + ch.fill(f"x{g}"))
                    act.wait_ge(S["past_in"], ONE + G * n + g + 1)
                    act.activation(past[:, g, :], tile[:, T:T + PAD], ACT.Copy).then_inc(S["past_out"], 1)
                return work

            def tanh_conv(g):
                def work(ch):
                    n = ch.c + 1
                    act.wait_ge(S["conv"], ONE + TAPS * (G * n + g + 1))
                    act.wait_ge(S["xs2"], ONE + G * n + max(g - 1, 0))
                    act.activation(conv_tanh[g % 2], conv[g % 2], ACT.Tanh, scale=0.5).then_inc(S["conv_tanh"], 1)
                return work

            def tanh_z(g):
                def work(ch):
                    act.wait_ge(s_filled, ONE + ch.fill(f"z{g}"))
                    act.wait_ge(s_read, ONE + ch.fill(f"z{g}") - 1)
                    act.activation(z_tanh[:, :], p_side[:, :], ACT.Tanh, scale=0.5).then_inc(S["z_tanh"], 1)
                return work

            def shared_tanh(ch):
                act.wait_ge(s_filled, ONE + ch.fill("shared_gate"))
                act.wait_ge(s_read, ONE + ch.fill("shared_gate") - 1)
                act.activation(shared_sig[:, :], p_side[:, :], ACT.Tanh, scale=0.5,
                               bias=half_gate_b[:, NE:NE + 1]).then_inc(S["sh_tanh"], 1)
                act.wait_ge(S["sh_tanh"], ONE + ch.c + 1)
                act.activation(shared_sig[:, :], shared_sig[:, :], ACT.Identity, bias=1.0).then_inc(S["sh_sig"], 1)

            def router_exp(ch):
                n = ch.c + 1
                act.wait_ge(s_read, ONE + ch.fill("logits"))
                act.wait_ge(S["aff"], ONE + n)
                act.activation(aff_e[:, :, :], logits[:, :, :], ACT.Exp, scale=-1.0).then_inc(S["aff_e"], 1)

            def take_dt(g):
                def work(ch):
                    n, (_, half) = ch.c + 1, ch.next_place()
                    act.wait_ge(s_filled, ONE + ch.fill(f"dt{g}"))
                    if g == 0:
                        act.wait_ge(S["delta"], ONE + n)
                    act.activation(sp_e[:, g, :], p_side[:, :], ACT.Abs, bias=dt_b[:, g:g + 1])\
                       .then_inc(S["sp_abs"], 1)
                    act.activation(delta[half][:, g, :], p_side[:, :], ACT.Relu, bias=dt_b[:, g:g + 1])\
                       .then_inc(s_read, 1)
                return work

            def softplus_exp(g):
                def work(ch):
                    n = ch.c + 1
                    act.wait_ge(S["sp_abs"], ONE + G * n + g + 1)
                    act.activation(sp_e[:, g, :], sp_e[:, g, :], ACT.Exp, scale=-1.0).then_inc(S["sp_e"], 1)
                return work

            def softplus_ln(ch):
                n = ch.c + 1
                act.wait_ge(S["xs2"], ONE + G * (n + 1))
                act.wait_ge(S["sp_e"], ONE + G * (n + 1))
                act.activation(sp_ln[:, :, :], sp_e[:, :, :], ACT.Ln, bias=1.0).then_inc(S["sp_ln"], 1)
                act.preload_act_table(ACT.Tanh)

            def take_weights(ch):
                n = ch.c + 1
                act.wait_ge(s_filled, ONE + ch.fill("weights"))
                act.wait_ge(s_w_stored, ONE + 64 * n)
                act.wait_ge(S["bias"], ONE + n)
                act.activation(weight_rows, p_side[0:2 * NE, :], ACT.Copy).then_inc(s_read, 1)

            table = {
                (0, "start"): [("post", take_out)],
                (0, "late"): [("own", y_init)],
                (3, "early"): [("pre", take_xnT(0))], (3, "late"): [("pre", take_xnT(1))],
                (4, "early"): [("own", tanh_z(0))], (4, "late"): [("pre", take_x(0))],
                (5, "early"): [("pre", tanh_conv(0))], (5, "late"): [("pre", take_x(1)), ("pre", router_exp)],
                (6, "early"): [("pre", tanh_conv(1))], (6, "late"): [("pre", take_x(2))],
                (7, "early"): [("pre", tanh_conv(2))], (7, "late"): [("pre", take_x(3))],
                (8, "early"): [("own", tanh_z(1)), ("pre", tanh_conv(3))], (8, "late"): [("own", shared_tanh)],
                (10, "early"): [("own", tanh_z(2))], (10, "late"): [("pre", take_dt(0))],
                (11, "early"): [("pre", softplus_exp(0))], (11, "late"): [("pre", take_dt(1))],
                (12, "early"): [("pre", softplus_exp(1))], (12, "late"): [("pre", take_dt(2))],
                (13, "early"): [("own", tanh_z(3)), ("pre", softplus_exp(2))], (13, "late"): [("pre", take_dt(3))],
                (14, "early"): [("pre", softplus_exp(3)), ("pre", take_weights)],
                (14, "late"): [("pre", softplus_ln)],
            }

            def split_high(s):
                k = s % 2
                act.wait_ge(s_raw_gu[k], 16 * (s // 2 + 1))
                act.wait_ge(s_raw_dn[k], 16 * (s // 2 + 1))
                act.activation(w_gu[k][:, 0, :, :], w_gu[k][:, 1, :, :].bitcast(F32), ACT.Copy)
                act.activation(w_dn[k][:, 0, :, :], w_dn[k][:, 1, :, :].bitcast(F32), ACT.Copy)\
                    .then_inc(s_w_hi, 1)

            def steps(ch):
                if ch is first_chunk:
                    split_high(0)
                for s in range(NS):
                    n = ch.c * NS + s

                    def decay(g):
                        act.wait_ge(s_scan, ONE + G * n + g)
                        act.activation(p_decay[:, :], delta[ch.half][:, g, :], ACT.Exp,
                                       scale=a_neg[:, s * G + g:s * G + g + 1]).then_inc(s_decay, 1)

                    def gate(j):
                        act.wait_ge(s_gate, ONE + EN * n + j + 1)
                        if not (ch is first_chunk and s == 0):
                            act.wait_ge(s_down, ONE + EN * (n - 1) + j + 1)
                        act.activation(act_tile[j][:, :], p_gate[:, :], ACT.Tanh, scale=0.5,
                                        bias=half_gate_b[:, s * EN + j:s * EN + j + 1]).then_inc(s_tanh, 1)
                        act.activation(gate_in[j][:, :], p_gate[:, :], ACT.Identity,
                                        bias=gate_b[:, s * EN + j:s * EN + j + 1]).then_inc(s_gate_in, 1)
                        act.wait_ge(s_tanh, ONE + EN * n + j + 1)
                        act.activation(act_tile[j][:, :], act_tile[j][:, :], ACT.Identity, bias=1.0)\
                           .then_inc(s_sig, 1)

                    def high(n, j):
                        act.wait_ge(s_hidden, ONE + EN * n + j + 1)
                        act.activation(hid_hi[j][:, :], act_tile[j][:, :], ACT.Copy).then_inc(s_hid_hi, 1)

                    beside(table, ch, s, "start")
                    if s == 0:
                        act.wait_ge(S["delta"], ONE + ch.c + 1)
                    decay(0)
                    if s > 0:
                        high(n - 1, 1)
                    gate(0)
                    decay(1)
                    decay(2)
                    gate(1)
                    decay(3)
                    high(n, 0)
                    beside(table, ch, s, "early")
                    act.wait_ge(s_scan, ONE + G * (n + 1))
                    act.activation(h_last[:, s, :], h[:, :, T - 1], ACT.Copy).then_inc(s_h_last, 1)
                    beside(table, ch, s, "late")
                    if s == NS - 1:
                        high(n, 1)
                    if ch is first_chunk and s + 1 < NS:
                        split_high(s + 1)

            all_chunks(act, alone(table), steps)

        @block.vector
        def _(dve):
            dve.wait_ge(s_setup, SETUP)
            consts = [
                dve.tensor_copy(pick[:, :, :], pick_raw),
                dve.tensor_scalar(half_gate_b[:, :], gate_b[:, :], 0.5, None, ALU.mult),
                dve.tensor_scalar(half_d[:, :], skip_d, 0.5, None, ALU.mult),
                dve.tensor_scalar(bc_wT[:, :, 0:NS], bc_wT[:, :, 0:NS], 0.25, None, ALU.mult),
                dve.tensor_scalar(bc_wT[:, :, NS:2 * NS], bc_wT[:, :, NS:2 * NS], 0.5, None, ALU.mult),
                dve.tensor_scalar(shared_dn[:, :], shared_dn[:, :], 0.5, None, ALU.mult),
                dve.tensor_copy(in_w[:, 0, :, :], in_w_raw[:, :, :]),
                dve.tensor_copy(shared_gu[:, 0, :], shared_gu_raw),
            ]
            for made in consts:
                made.then_inc(s_const_dve, 1)
            dve.wait_ge(s_a_exp, 1)
            dve.tensor_scalar(a_neg[:, :], a_exp, -1.0, None, ALU.mult).then_inc(s_const_dve, 1)
            dve.wait_ge(s_const_dve, len(consts))
            dve.tensor_tensor(in_w[:, 1, :, :], in_w_raw[:, :, :], in_w[:, 0, :, :].bitcast(F32),
                              ALU.subtract).then_inc(s_const_dve, 1)
            dve.tensor_tensor(shared_gu[:, 1, :], shared_gu_raw, shared_gu[:, 0, :].bitcast(F32),
                              ALU.subtract).then_inc(s_const_dve, 1)
            for g in range(G):
                dve.wait_ge(s_fused, g + 1)
                dve.tensor_scalar(dt_fused[:, g, :], fused_banks[g][:, :], 0.5, None, ALU.mult)\
                   .then_inc(s_fused_kept, 1)

            def yz(ch):
                dve.wait_ge(s_y, ONE + 2 * NS * ch.c)
                dve.wait_ge(s_read, ONE + ch.fills_before)
                for g in range(G):
                    dve.scalar_tensor_tensor(out=z_gate[:, g, :], in0=y[:, g, :], scalar=0.5, in1=z_gate[:, g, :],
                                             op0=ALU.mult, op1=ALU.mult).then_inc(S["yz"], 1)

            def norm_stats(ch):
                n = ch.c + 1
                dve.wait_ge(s_x_ln, ONE + 16 * (n + 1))
                dve.wait_ge(S["mean_var"], ONE + TT * n)
                apart(dve)
                for t in range(TT):
                    dve.bn_stats(stats[:, t, :], x_ln[:, t, :]).then_inc(S["stats"], 1)

            def norm_aggr(ch):
                n = ch.c + 1
                dve.wait_ge(S["var_eps"], ONE + n)
                dve.wait_ge(S["xn"], ONE + TT * n)
                dve.wait_ge(S["stats"], ONE + TT * (n + 1))
                apart(dve)
                for t in range(TT):
                    dve.bn_aggr(mean_var[:, t, :], stats[:, t, :]).then_inc(S["mean_var"], 1)

            def norm(ch):
                n = ch.c + 1
                dve.wait_ge(S["rstd"], ONE + n + 1)
                dve.wait_ge(S["mean_var"], ONE + TT * (n + 1))
                for t in range(TT):
                    dve.tensor_scalar(x_ln[:, t, :], x_ln[:, t, :], mean_var[:, t, 0:1], rstd[:, t:t + 1],
                                      ALU.subtract, ALU.mult).then_inc(S["xn"], 1)

            def low_x(k):
                def work(ch):
                    tile = xnT[ch.next_place()[1]]
                    dve.wait_ge(S["xnT_hi"], ONE + KM * (ch.c + 1) + k + 1)
                    dve.tensor_tensor(tile[:, 1, k, :], p_side[:, :], tile[:, 0, k, :].bitcast(F32), ALU.subtract)\
                       .then_inc(s_read, 1)
                return work

            def add_out(m):
                def work(ch):
                    dve.wait_ge(s_filled, ONE + ch.fill(f"out_proj{m}"))
                    dve.wait_ge(S["o_sb"], ONE + KM * (ch.c - 1) + m + 1)
                    dve.tensor_tensor(o_sb[:, m, :], p_side[:, :], o_sb[:, m, :], ALU.add).then_inc(s_read, 1)
                return work

            def add_residual(q):
                def work(ch):
                    dve.wait_ge(s_filled, ONE + ch.fill(f"tokens{q}"))
                    dve.wait_ge(s_x_res, ONE + 16 * ch.c)
                    dve.wait_ge(s_out, ONE + 16 * (ch.c - 1))
                    dve.tensor_tensor(o_tok[:, 2 * q:2 * q + 2, :],
                                      p_side[:, :].rearrange("p (t d) -> p t d", d=DM),
                                      x_res[:, 2 * q:2 * q + 2, :], ALU.add).then_inc(s_read, 1)
                return work

            def gate_z(g):
                def work(ch):
                    dve.wait_ge(S["z_tanh"], ONE + G * ch.c + g + 1)
                    dve.wait_ge(s_filled, ONE + ch.fill(f"z{g}"))
                    dve.scalar_tensor_tensor(out=z_gate[:, g, :], in0=z_tanh[:, :], scalar=1.0, in1=p_side[:, :],
                                             op0=ALU.add, op1=ALU.mult).then_inc(s_read, 1)
                return work

            def take_logits(ch):
                n = ch.c + 1
                dve.wait_ge(s_filled, ONE + ch.fill("logits"))
                dve.wait_ge(S["aff_e"], ONE + n)
                dve.wait_ge(S["chosen"], ONE + n)
                dve.tensor_copy(logits[:, :, :], p_side[:, 0:TT * NE].rearrange("p (t e) -> p t e", e=NE))\
                   .then_inc(s_read, 1)

            def convolve(g):
                def work(ch):
                    n, tile = ch.c + 1, x_pad[g % 2]
                    dve.wait_ge(s_read, ONE + ch.fill(f"x{g}"))
                    dve.wait_ge(S["past_in"], ONE + G * n + g + 1)
                    dve.wait_ge(S["xs2"], ONE + G * n + max(g - 1, 0))
                    dve.wait_ge(S["sp_sum"], ONE + n)
                    for tap in range(TAPS):
                        window = tile[:, tap:tap + T]
                        if tap == 0:
                            dve.tensor_scalar(conv[g % 2], window, conv_w[:, g, 0:1], conv_b[:, g:g + 1],
                                              ALU.mult, ALU.add).then_inc(S["conv"], 1)
                        else:
                            dve.wait_ge(S["conv"], ONE + TAPS * (G * n + g) + tap)
                            dve.scalar_tensor_tensor(out=conv[g % 2], in0=window, scalar=conv_w[:, g, tap:tap + 1],
                                                     in1=conv[g % 2], op0=ALU.mult, op1=ALU.add)\
                               .then_inc(S["conv"], 1)
                return work

            def gate_x(g):
                def work(ch):
                    n = ch.c + 1
                    dve.wait_ge(S["conv_tanh"], ONE + G * n + g + 1)
                    dve.wait_ge(S["y_init"], ONE + G * n)
                    dve.wait_ge(S["du2"], ONE + n)
                    dve.wait_ge(s_filled, ONE + ch.fills_before)
                    dve.scalar_tensor_tensor(out=xs2[:, g, :], in0=conv_tanh[g % 2], scalar=1.0, in1=conv[g % 2],
                                             op0=ALU.add, op1=ALU.mult).then_inc(S["xs2"], 1)
                return work

            def find_top(ch):
                n = ch.c + 1
                dve.wait_ge(s_read, ONE + ch.fill("logits"))
                dve.wait_ge(S["without_top"], ONE + TT * n)
                apart(dve)
                for t in range(TT):
                    dve.max(top[:, t, :], logits[:, t, :]).then_inc(S["top"], 1)

            def take_top(ch):
                n = ch.c + 1
                dve.wait_ge(S["top"], ONE + TT * (n + 1))
                dve.wait_ge(S["chosen"], ONE + n)
                apart(dve)
                for t in range(TT):
                    dve.match_replace(without_top[:, t, :], in_to_replace=top[:, t, :], in_values=logits[:, t, :],
                                      imm_value=BELOW_ALL).then_inc(S["without_top"], 1)

            def sigmoid(ch):
                n = ch.c + 1
                dve.wait_ge(S["aff_e"], ONE + n + 1)
                dve.tensor_scalar(aff_e[:, :, :], aff_e[:, :, :], 1.0, None, ALU.add).then_inc(S["aff_d"], 1)
                dve.wait_ge(S["without_top"], ONE + TT * (n + 1))
                dve.wait_ge(S["aff_top"], ONE + n)
                dve.tensor_tensor(chosen[:, :, :], without_top[:, :, :], logits[:, :, :], ALU.not_equal)\
                   .then_inc(S["chosen"], 1)
                dve.wait_ge(S["aff_d"], ONE + n + 1)
                dve.reciprocal(aff[:, :, :], aff_e[:, :, :]).then_inc(S["aff"], 1)

            def sum_top(ch):
                n = ch.c + 1
                dve.wait_ge(S["aff"], ONE + n + 1)
                dve.wait_ge(S["chosen"], ONE + n + 1)
                dve.wait_ge(S["weight_lo"], ONE + n)
                dve.tensor_tensor(aff_top[:, :, :], aff[:, :, :], chosen[:, :, :], ALU.mult).then_inc(S["aff_top"], 1)
                dve.wait_ge(S["aff_top"], ONE + n + 1)
                dve.tensor_reduce(aff_sum[:, :], aff_top[:, :, :], AX.X, ALU.add).then_inc(S["aff_sum"], 1)

            def invert_sum(ch):
                n = ch.c + 1
                dve.wait_ge(S["aff_sum"], ONE + n + 1)
                dve.tensor_scalar(aff_sum[:, :], aff_sum[:, :], SUM_EPS, None, ALU.add).then_inc(S["aff_sum_eps"], 1)
                dve.wait_ge(S["aff_sum_eps"], ONE + n + 1)
                dve.reciprocal(aff_inv[:, :], aff_sum[:, :]).then_inc(S["aff_inv"], 1)

            def weigh(ch):
                n = ch.c + 1
                dve.wait_ge(S["aff_inv"], ONE + n + 1)
                dve.wait_ge(S["weight_lo"], ONE + n)
                dve.tensor_tensor(aff_top[:, :, :], aff_top[:, :, :],
                                  aff_inv[:, :].rearrange("p (t o) -> p t o", o=1).broadcast_to([P, TT, NE]),
                                  ALU.mult).then_inc(S["weight"], 1)

            def split_weights(ch):
                n = ch.c + 1
                dve.wait_ge(S["weight"], ONE + n + 1)
                dve.wait_ge(s_filled, ONE + ch.fills_before)
                dve.tensor_copy(weight_split[:, :, 0, :], aff_top[:, :, :]).then_inc(S["weight_hi"], 1)
                dve.wait_ge(S["weight_hi"], ONE + n + 1)
                dve.tensor_tensor(weight_split[:, :, 1, :], aff_top[:, :, :], weight_split[:, :, 0, :].bitcast(F32),
                                  ALU.subtract).then_inc(S["weight_lo"], 1)

            def shared_silu(ch):
                dve.wait_ge(S["sh_sig"], ONE + ch.c + 1)
                dve.wait_ge(S["sh_down"], ONE + ch.c)
                dve.scalar_tensor_tensor(out=shared_sig[:, :], in0=p_side[:, :], scalar=gate_b[:, NE:NE + 1],
                                         in1=shared_sig[:, :], op0=ALU.add, op1=ALU.mult).then_inc(s_read, 1)

            def shared_times_up(ch):
                dve.wait_ge(s_filled, ONE + ch.fill("shared_up"))
                dve.wait_ge(s_read, ONE + ch.fill("shared_gate"))
                dve.scalar_tensor_tensor(out=shared_up, in0=p_side[:, :], scalar=up_b[:, NE:NE + 1],
                                         in1=shared_sig[:, :], op0=ALU.add, op1=ALU.mult).then_inc(s_read, 1)

            def split_bc(ch):
                n = ch.c + 1
                dve.wait_ge(s_filled, ONE + ch.fill("bc"))
                dve.wait_ge(S["past_out"], ONE + G * (n + 1))
                dve.wait_ge(S["conv"], ONE + TAPS * G * (n + 1))
                dve.tensor_copy(bc_hi[:, :], p_side[0:2 * NS, :]).then_inc(S["bc_hi"], 1)
                dve.wait_ge(S["bc_hi"], ONE + n + 1)
                dve.tensor_tensor(bc_lo[:, :], p_side[0:2 * NS, :], bc_hi[:, :].bitcast(F32), ALU.subtract)\
                   .then_inc(s_read, 1)

            def softplus_back(ch):
                n = ch.c + 1
                if ch is not start:
                    dve.wait_ge(s_out, ONE + 16 * ch.c)
                    dve.wait_ge(S["delta"], ONE + n)
                for g in range(G):
                    dve.wait_ge(S["sp_e"], ONE + G * n + g + 1)
                    dve.tensor_scalar(sp_back[:, g, :], sp_e[:, g, :], 1.0, 1.0, ALU.add, ALU.subtract)\
                       .then_inc(S["sp_back"], 1)

            def softplus_sum(ch):
                n, (_, half) = ch.c + 1, ch.next_place()
                dve.wait_ge(S["sp_ln"], ONE + n + 1)
                dve.wait_ge(s_read, ONE + ch.fill("dt3"))
                dve.tensor_tensor(delta[half][:, :, :], delta[half][:, :, :], sp_ln[:, :, :], ALU.add)\
                   .then_inc(S["sp_sum"], 1)

            def softplus_delta(ch):
                n, (_, half) = ch.c + 1, ch.next_place()
                dve.wait_ge(S["sp_rest"], ONE + n + 1)
                dve.wait_ge(S["sp_sum"], ONE + n + 1)
                dve.tensor_tensor(delta[half][:, :, :], delta[half][:, :, :], sp_back[:, :, :], ALU.add)\
                   .then_inc(S["delta"], 1)

            def delta_x(ch):
                n, (_, half) = ch.c + 1, ch.next_place()
                dve.wait_ge(S["delta"], ONE + n + 1)
                dve.wait_ge(S["xs2"], ONE + G * (n + 1))
                if ch is not start:
                    dve.wait_ge(s_u_in, ONE + 2 * NS * n)
                dve.tensor_tensor(du2[:, :, :], delta[half][:, :, :], xs2[:, :, :], ALU.mult)\
                   .then_inc(S["du2"], 1)

            table = {
                (0, "early"): [("post", yz)], (0, "late"): [("pre", norm_stats)],
                (1, "early"): [("pre", norm_aggr)], (1, "late"): [("post", add_out(0))],
                (2, "early"): [("pre", norm)], (2, "late"): [("post", add_out(1))],
                (3, "early"): [("pre", low_x(0))], (3, "late"): [("pre", low_x(1))],
                (4, "early"): [("own", gate_z(0))], (4, "late"): [("pre", convolve(0))],
                (5, "early"): [("pre", take_logits), ("pre", gate_x(0))], (5, "late"): [("pre", convolve(1))],
                (6, "early"): [("post", add_residual(0)), ("pre", gate_x(1))],
                (6, "late"): [("pre", find_top), ("pre", convolve(2))],
                (7, "early"): [("post", add_residual(1)), ("pre", gate_x(2))],
                (7, "late"): [("pre", take_top), ("pre", convolve(3))],
                (8, "early"): [("own", gate_z(1)), ("pre", gate_x(3))],
                (8, "late"): [("own", shared_silu), ("pre", sigmoid)],
                (9, "early"): [("own", shared_times_up), ("pre", sum_top)], (9, "late"): [("pre", split_bc)],
                (10, "early"): [("own", gate_z(2)), ("pre", invert_sum)], (10, "late"): [("pre", weigh)],
                (11, "early"): [("pre", split_weights)],
                (13, "early"): [("own", gate_z(3))],
                (14, "early"): [("pre", softplus_back)],
                (15, "early"): [("pre", softplus_sum)],
                (15, "late"): [("pre", softplus_delta), ("pre", delta_x)],
            }

            def steps(ch):
                if ch.half == 0:
                    dve.wait_ge(s_h_last, ONE + NS * ch.c)
                    apart(dve)
                    dve.memset(h_last[:, :, :], 0.0).then_inc(S["h_zero"], 1)
                dve.wait_ge(S["h_zero"], ONE + ch.b + 1)
                dve.wait_ge(S["du2"], ONE + ch.c + 1)
                for s in range(NS):
                    n = ch.c * NS + s

                    def all_blocks(psum, blocks=G):
                        return psum[:, :].rearrange("p (o t) -> p o t", o=1).broadcast_to([P, blocks, T])

                    def scan(g):
                        dve.wait_ge(s_decay, ONE + G * n + g + 1)
                        dve.tensor_tensor_scan(h[:, g, :], p_decay[:, :], u_in[:, g, :], h_last[:, s, g:g + 1],
                                               ALU.mult, ALU.add).then_inc(s_scan, 1)

                    def times_up(j):
                        dve.wait_ge(s_up, ONE + EN * n + j + 1)
                        dve.wait_ge(s_silu, ONE + EN * n + j + 1)
                        dve.scalar_tensor_tensor(out=act_tile[j][:, :], in0=p_up[:, :],
                                                 scalar=up_b[:, s * EN + j:s * EN + j + 1], in1=act_tile[j][:, :],
                                                 op0=ALU.add, op1=ALU.mult).then_inc(s_act_up, 1)

                    def times_weight(j):
                        dve.wait_ge(s_wb, ONE + EN * n + j + 1)
                        dve.wait_ge(s_act_up, ONE + EN * n + j + 1)
                        dve.scalar_tensor_tensor(out=act_tile[j][:, :], in0=act_tile[j][:, :], scalar=0.5, in1=p_w[:, :],
                                                 op0=ALU.mult, op1=ALU.mult).then_inc(s_hidden, 1)

                    def inputs(part):
                        blocks = slice(2 * part, 2 * part + 2)
                        dve.tensor_tensor(u_in[:, blocks, :], du2[:, blocks, :], all_blocks(p_bc, 2), ALU.mult)\
                           .then_inc(s_u_in, 1)

                    dve.wait_ge(s_b, ONE + n + 1)
                    dve.wait_ge(s_hc, ONE + n)
                    dve.wait_ge(s_h_last, ONE + n)
                    inputs(0)
                    dve.wait_ge(s_u_in, ONE + 2 * n + 1)
                    scan(0)
                    inputs(1)
                    scan(1)
                    dve.wait_ge(s_u_in, ONE + 2 * n + 2)
                    times_up(0)
                    scan(2)
                    times_weight(0)
                    scan(3)
                    beside(table, ch, s, "early")
                    dve.wait_ge(s_scan, ONE + G * (n + 1))
                    dve.wait_ge(s_c, ONE + n + 1)
                    dve.wait_ge(s_y, ONE + 2 * n)
                    dve.tensor_tensor(hc[:, :, :], h[:, :, :], all_blocks(p_bc), ALU.mult).then_inc(s_hc, 1)
                    times_up(1)
                    times_weight(1)
                    beside(table, ch, s, "late")

            all_chunks(dve, alone(table), steps)

        @block.tensor
        def _(pe):
            pe.wait_ge(s_setup, SETUP)
            for g in range(G):
                for j in range(G):
                    mm = pe.matmul(fused_banks[g][:, :], x_w[:, j, g * P:(g + 1) * P], dt_wT[:, j, :],
                                   start=(j == 0), stop=(j == G - 1))
                mm.then_inc(s_fused, 1)
            pe.wait_ge(s_const_dve, 11)
            pe.wait_ge(s_const_pool, 3)
            pe.wait_ge(s_fused_kept, G)

            def in_parts(out, factors, start=True, stop=True):
                passes = [(w[:, i], x[:, j]) for w, x in factors for i, j in ((0, 0), (0, 1), (1, 0))]
                for at, (w, x) in enumerate(passes):
                    mm = pe.matmul(out[:, :], w, x, start=(start and at == 0),
                                   stop=(stop and at == len(passes) - 1))
                return mm

            def fill(name, product):
                def work(ch):
                    pe.wait_ge(s_read, ONE + ch.fill(name) - 1)
                    product(ch).then_inc(s_filled, 1)
                return work

            def biases(ch):
                pe.wait_ge(s_read, ONE + ch.fills_before)
                pe.wait_ge(S["o_sb"], ONE + KM * ch.c)
                for m in range(KM):
                    mm = pe.matmul(p_out[m][:, :], down_b[:, m * P:(m + 1) * P], weight_rows,
                                   start=True, stop=False)
                mm.then_inc(S["bias"], 1)

            def shared_down(ch):
                pe.wait_ge(s_read, ONE + ch.fill("shared_up"))
                for m in range(KM):
                    mm = pe.matmul(p_out[m][:, :], shared_dn[:, m * P:(m + 1) * P],
                                   shared_up, start=False, stop=False)
                mm.then_inc(S["sh_down"], 1)

            def out_proj(m):
                def product(ch):
                    for g in range(G):
                        pe.wait_ge(S["yz"], ONE + G * (ch.c - 1) + g + 1)
                        mm = pe.matmul(p_side[:, :], out_wT[:, g, m * P:(m + 1) * P], z_gate[:, g, :],
                                       start=(g == 0), stop=(g == G - 1))
                    return mm
                return product

            def transpose_x(k):
                def product(ch):
                    for t in range(TT):
                        pe.wait_ge(S["xn"], ONE + TT * (ch.c + 1) + t + 1)
                        mm = pe.transpose(p_side[:, t * P:(t + 1) * P], x_ln[:, t, k * P:(k + 1) * P], ident[:, :])
                    return mm
                return product

            def tokens(q):
                def product(ch):
                    pe.wait_ge(s_read, ONE + ch.fill("out_proj1"))
                    for t in range(2):
                        for m in range(KM):
                            mm = pe.transpose(p_side[:, t * DM + m * P:t * DM + (m + 1) * P],
                                              o_sb[:, m, (2 * q + t) * P:(2 * q + t + 1) * P], ident[:, :])
                    return mm
                return product

            def in_proj(m, other_half):
                def product(ch):
                    tokens_T = xnT[ch.next_place()[1] if other_half else ch.half]
                    return in_parts(p_side, [(in_w[:, :, k, m * P:(m + 1) * P], tokens_T[:, :, k, :])
                                             for k in range(KM)])
                return product

            def shared(i):
                def product(ch):
                    return in_parts(p_side, [(shared_gu[:, :, (2 * i + k) * NI:(2 * i + k + 1) * NI],
                                              xnT[ch.half][:, :, k, :]) for k in range(KM)])
                return product

            def router(ch):
                half = ch.next_place()[1]
                for t in range(TT):
                    out = p_side[:, t * NE:(t + 1) * NE]
                    for k in range(KM):
                        for part in range(PARTS):
                            pe.matmul(out, xnT[half][:, part, k, t * P:(t + 1) * P].bitcast(F32), router_w[:, k, :],
                                      start=(k == 0 and part == 0), stop=False)
                    mm = pe.matmul(out, ones_row[:, :], router_b[:, :], start=False, stop=True)
                return mm

            def b_and_c(ch):
                for g in range(G):
                    pe.wait_ge(S["xs2"], ONE + G * (ch.c + 1) + g + 1)
                    mm = pe.matmul(p_side[0:2 * NS, :], bc_wT[:, g, :], xs2[:, g, :],
                                   start=(g == 0), stop=(g == G - 1))
                return mm

            def dt_proj(m):
                def product(ch):
                    for g in range(G):
                        mm = pe.matmul(p_side[:, :], dt_fused[:, g, m * P:(m + 1) * P], xs2[:, g, :],
                                       start=(g == 0), stop=(g == G - 1))
                    return mm
                return product

            def weights(ch):
                pe.wait_ge(S["weight_lo"], ONE + ch.c + 2)
                apart(pe)
                for t in range(TT):
                    mm = pe.transpose(p_side[0:2 * NE, t * P:(t + 1) * P],
                                      weight_split[:, t, :, :].bitcast(F32).rearrange("p a e -> p (a e)"),
                                      ident[:, :])
                return mm

            products = {
                "out_proj0": out_proj(0), "out_proj1": out_proj(1), "xnT0": transpose_x(0), "xnT1": transpose_x(1),
                "logits": router, "tokens0": tokens(0), "tokens1": tokens(1), "shared_gate": shared(0),
                "shared_up": shared(1), "bc": b_and_c, "weights": weights,
                **{f"x{g}": in_proj(g, True) for g in range(G)}, **{f"z{g}": in_proj(G + g, False) for g in range(G)},
                **{f"dt{g}": dt_proj(g) for g in range(G)},
            }
            table = {at: [(kind, fill(name, products[name]))] for at, (kind, name) in FILLS.items()}
            table[(0, "start")] = [("own", biases)]
            table[(14, "A")] = [("own", shared_down)]

            def sides(ch):
                alone(table)(ch)
                if ch is start:
                    pe.wait_ge(s_row_b0, ONE + 16)
                    pe.matmul(p_bc[:, :], pick[0:2, 0, :], row_b0[:, :], start=True, stop=True).then_inc(s_b, 1)

            def steps(ch):
                for s in range(NS):
                    n, k = ch.c * NS + s, s % 2
                    turn = ch.c * (NS // 2) + s // 2

                    def gate(j):
                        pe.wait_ge(s_gate_in, ONE + EN * n + j)
                        in_parts(p_gate, [(w_gu[k][:, :, j, kk * NI:(kk + 1) * NI], xnT[ch.half][:, :, kk, :])
                                          for kk in range(KM)]).then_inc(s_gate, 1)

                    def up(j):
                        pe.wait_ge(s_act_up, ONE + EN * n + j)
                        in_parts(p_up, [(w_gu[k][:, :, j, (KM + kk) * NI:(KM + kk + 1) * NI],
                                         xnT[ch.half][:, :, kk, :]) for kk in range(KM)]).then_inc(s_up, 1)

                    def spread_weight(j):
                        pe.wait_ge(s_hidden, ONE + EN * n + j)
                        pe.matmul(p_w[:, :], pick[:, 2 + j, :], rows[k][:, :], start=True, stop=True)\
                          .then_inc(s_wb, 1)

                    def down(n, s, j):
                        last = s == NS - 1 and j == EN - 1
                        pe.wait_ge(s_hid_lo, ONE + EN * n + j + 1)
                        for m in range(KM):
                            for part, hid in ((0, hid_hi[j][:, :]), (0, hid_lo[j][:, :]), (1, hid_hi[j][:, :])):
                                mm = pe.matmul(p_out[m][:, :], w_dn[s % 2][:, part, j, m * P:(m + 1) * P], hid,
                                               start=False, stop=(last and part == 1))
                        mm.then_inc(s_down, 1)

                    beside(table, ch, s, "start")
                    if ch is first_chunk:
                        pe.wait_ge(s_w_lo, s + 1)
                    else:
                        pe.wait_ge(s_wgu[k], ONE + 16 * (turn + 1 - NS // 2))
                    gate(0)
                    up(0)
                    if s > 0:
                        down(n - 1, s - 1, 1)
                    pe.wait_ge(s_rows[k], ONE + 16 * (turn + 1))
                    pe.wait_ge(s_u_in, ONE + 2 * (n + 1))
                    pe.matmul(p_bc[:, :], pick[:, 1, :], rows[k][:, :], start=True, stop=True).then_inc(s_c, 1)
                    spread_weight(0)
                    gate(1)
                    up(1)
                    spread_weight(1)
                    beside(table, ch, s, "A")
                    if ch is not first_chunk:
                        pe.wait_ge(s_wdn[k], ONE + 16 * (turn + 1 - NS // 2))
                    down(n, s, 0)
                    pe.wait_ge(s_hc, ONE + n + 1)
                    if s < NS - 1 or "pre" not in ch.kinds:
                        pe.matmul(p_bc[:, :], pick[:, 0, :], rows[k][:, :], start=True, stop=True).then_inc(s_b, 1)
                    else:
                        pe.wait_ge(s_row_b0, ONE + 16 * (ch.c + 2))
                        pe.matmul(p_bc[:, :], pick[0:2, 0, :], row_b0[:, :], start=True, stop=True).then_inc(s_b, 1)
                    beside(table, ch, s, "B")
                    if s == NS - 1:
                        down(n, s, 1)

            all_chunks(pe, sides, steps)


def kernel(**inputs):
    import numpy as np
    import concourse.bacc as bacc
    from concourse.bass_utils import run_bass_kernel_spmd

    a = {k.split("_", 2)[2]: np.asarray(v) for k, v in inputs.items()}

    def blocks(w):
        return w.reshape(w.shape[0] // P, P, -1).transpose(1, 0, 2)

    def columns(v):
        return v.reshape(-1, P).T

    def expert(gate, up, down):
        lead = gate.shape[:-2]
        parts = [w.reshape(*lead, KM, P, NI)[..., k, :, :] for w in (gate, up) for k in range(KM)]
        return np.concatenate(parts, axis=-1), down

    x_proj = a["x_proj_w"]
    turned = np.roll(np.arange(NS), -1)
    bc = np.concatenate([x_proj[DI:DI + NS][turned], x_proj[DI + NS:]], axis=0)
    gu, dn = expert(a["Wg"], a["Wu"], a["Wd"])
    pairs = np.arange(NE).reshape(EN, NS).T
    gu_s, dn_s = expert(a["Wg_s"], a["Wu_s"], a["Wd_s"])
    order = pairs.reshape(-1)
    arrays = {
        "x": a["x"],
        "in_wT": blocks(a["in_proj_w"].T), "bc_wT": blocks(bc.T), "out_wT": blocks(a["out_proj_w"].T),
        "x_w": blocks(x_proj[:DI]), "dt_wT": blocks(a["dt_proj_w"].T),
        "shared_w": np.concatenate([gu_s, dn_s], axis=-1),
        "router_w": blocks(a["Wr"]), "router_b": a["br"].reshape(1, NE),
        "down_b": a["bd"], "shared_down_b": columns(a["bd_s"]),
        "conv_w": blocks(a["conv_w"].reshape(DI, TAPS)), "conv_b": columns(a["conv_b"]),
        "dt_b": columns(a["dt_proj_b"]), "skip_d": columns(a["D"]),
        "a_log": blocks(a["A_log"]).transpose(0, 2, 1).reshape(P, NS * G),
        "gate_b": np.concatenate([a["bg"][order], a["bg_s"].reshape(1, NI)]).T,
        "up_b": np.concatenate([a["bu"][order], a["bu_s"].reshape(1, NI)]).T,
        "w_gu": gu[pairs].transpose(0, 2, 1, 3), "w_dn": dn[pairs].transpose(0, 2, 1, 3),
        "ident": np.eye(P, dtype=np.float32),
        "pick": np.repeat(np.repeat(np.eye(ROWS // 2, dtype=np.float32), 2, axis=0)[:, :, None], P, axis=2),
    }
    nc = bacc.Bacc("TRN2", target_bir_lowering=False, num_devices=1)
    feed, io = {}, {}
    for name, v in arrays.items():
        v = np.ascontiguousarray(v)
        feed[f"in_{name}"] = v
        io[name] = nc.dram_tensor(f"in_{name}", v.shape, mybir.dt.from_np(v.dtype), kind="ExternalInput").ap()
    io["out"] = nc.dram_tensor("out_y", (BATCH, SEQ, DM), F32, kind="ExternalOutput").ap()
    build_program(nc, io)
    result = run_bass_kernel_spmd(nc, [feed], core_ids=[0])
    return result.results[0]["out_y"]
```

```python
from contextlib import ExitStack

import concourse.bass as bass
from concourse import mybir

F32 = mybir.dt.float32
F32R = mybir.dt.float32r
ALU = mybir.AluOpType
ACT = mybir.ActivationFunctionType
AX = mybir.AxisListType

P = 128
BATCH, SEQ, DM = 4, 1024, 256
T = 512
TT = T // P
HALVES = SEQ // T
CHUNKS = BATCH * HALVES
KM = DM // P
DI = 512
G = DI // P
NS = 16
TAPS = 4
PAD = TAPS - 1
NE = 32
EN = NE // NS
TOPK = 8
NI = 128
PARTS = 2
ROWS = 8
LN_EPS, SUM_EPS = 1e-5, 1e-9
BELOW_ALL = -3.3e38


def build_program(nc, io):
    with ExitStack() as ctx:
        def sb(name, shape, dt=F32):
            return ctx.enter_context(nc.sbuf_tensor(name, shape, dt))

        def bank(name):
            return ctx.enter_context(nc.psum_tensor(name, [P, T], F32))

        def sem(name):
            return ctx.enter_context(nc.semaphore(name))

        in_w = sb("in_w", [P, PARTS, KM, 2 * DI], F32R)
        dt_fused = sb("dt_fused", [P, G, DI])
        bc_wT = sb("bc_wT", [P, G, 2 * NS])
        out_wT = sb("out_wT", [P, G, DM])
        shared_gu = sb("shared_gu", [P, PARTS, 4 * NI], F32R)
        shared_dn = sb("shared_dn", [P, 2 * NI])
        router_w = sb("router_w", [P, KM, NE])
        router_b = sb("router_b", [1, NE])
        ones_row = sb("ones_row", [1, P])
        down_b = sb("down_b", [2 * NE, DM])
        shared_down_b = sb("shared_down_b", [P, KM])
        conv_w = sb("conv_w", [P, G, TAPS])
        conv_b = sb("conv_b", [P, G])
        dt_b = sb("dt_b", [P, G])
        a_neg = sb("a_neg", [P, NS * G])
        half_d = sb("half_d", [P, G])
        gate_b = sb("gate_b", [P, NE + 1])
        half_gate_b = sb("half_gate_b", [P, NE + 1])
        up_b = sb("up_b", [P, NE + 1])
        ident = sb("ident", [P, P])
        pick = sb("pick", [ROWS, ROWS // 2, P], F32R)
        minus_half = sb("minus_half", [P, TT])
        no_past = sb("no_past", [P, G, PAD])

        x_ln = sb("x_ln", [P, TT, DM])
        x_res = sb("x_res", [P, TT, DM])
        stats = sb("stats", [P, TT, 6])
        mean_var = sb("mean_var", [P, TT, 2])
        var_eps = sb("var_eps", [P, TT])
        rstd = sb("rstd", [P, TT])
        xnT = [sb(f"xnT{i}", [P, PARTS, KM, T], F32R) for i in range(2)]
        logits = sb("logits", [P, TT, NE])
        top = sb("top", [P, TT, TOPK])
        without_top = sb("without_top", [P, TT, NE])
        chosen = sb("chosen", [P, TT, NE])
        aff_e = sb("aff_e", [P, TT, NE])
        aff = sb("aff", [P, TT, NE])
        aff_top = sb("aff_top", [P, TT, NE])
        aff_sum = sb("aff_sum", [P, TT])
        aff_inv = sb("aff_inv", [P, TT])
        weight_split = sb("weight_split", [P, TT, 2, NE], F32R)
        weight_rows = x_res[0:2 * NE, TT // 2:TT, :].rearrange("p a d -> p (a d)")
        x_pad = [sb(f"x_pad{i}", [P, PAD + T]) for i in range(2)]
        bc_hi, bc_lo = (tile[0:2 * NS, 0:T].bitcast(F32R) for tile in x_pad)
        past = sb("past", [P, G, PAD])
        z_tanh = sb("z_tanh", [P, T])
        shared_sig = z_tanh
        z_gate = sb("z_gate", [P, G, T])
        scratch = sb("scratch", [P, G, T])
        conv = [scratch[:, i, :] for i in range(2)]
        conv_tanh = [scratch[:, 2 + i, :] for i in range(2)]
        sp_ln = scratch
        xs2 = sb("xs2", [P, G, T])
        sp_e = sb("sp_e", [P, G, T])
        delta = [sb(f"delta{i}", [P, G, T]) for i in range(2)]
        du2 = sb("du2", [P, G, T])
        shared_up = x_res[:, 0:TT // 2, :].rearrange("p a d -> p (a d)")
        o_area = sb("o_area", [P, G, T])
        o_sb = o_area[:, 0:KM, :]
        o_tok = o_area[:, KM:G, :].rearrange("p a (b d) -> p (a b) d", d=DM)
        sp_back = o_area

        w_gu = [sb(f"w_gu{i}", [P, PARTS, EN, 4 * NI], F32R) for i in range(2)]
        w_dn = [sb(f"w_dn{i}", [P, PARTS, EN, DM], F32R) for i in range(2)]
        rows = [sb(f"rows{i}", [ROWS, T], F32R) for i in range(2)]
        row_b0 = sb("row_b0", [2, T], F32R)
        h = sb("h", [P, G, T])
        u_in = h
        h_last = sb("h_last", [P, NS, G])
        hc = sb("hc", [P, G, T])
        y = sb("y", [P, G, T])
        act_tile = [sb(f"act_tile{i}", [P, T]) for i in range(EN)]
        gate_in = [sb(f"gate_in{i}", [P, T]) for i in range(EN)]
        hid_hi = [sb(f"hid_hi{i}", [P, T], F32R) for i in range(EN)]
        hid_lo = [sb(f"hid_lo{i}", [P, T], F32R) for i in range(EN)]
        pick_raw = y[0:ROWS, :, 0:P]
        a_exp = h[:, 0, 0:NS * G]
        a_log = h[:, 2, 0:NS * G]
        skip_d = h[:, 1, 0:G]
        x_w, dt_wT = sp_e, hc
        in_w_raw = scratch[:, :, :].rearrange("p (k a) t -> p k (a t)", k=KM)
        shared_gu_raw = xs2[:, 0, :]

        p_gate = bank("p_gate")
        p_up = bank("p_up")
        p_out = [bank(f"p_out{i}") for i in range(KM)]
        p_bc = bank("p_bc")
        p_w = bank("p_w")
        p_decay = bank("p_decay")
        p_side = bank("p_side")

        fused_banks = [p_gate, p_up, p_w, p_decay]

        row_store = [nc.dram_tensor(f"row_store{i}", [NS, ROWS, T], F32).ap() for i in range(HALVES)]
        gu_store = nc.dram_tensor("gu_store", [NS, P, PARTS, EN, 4 * NI], F32).ap()
        dn_store = nc.dram_tensor("dn_store", [NS, P, PARTS, EN, DM], F32).ap()

        s_setup = sem("s_setup")
        s_ident = sem("s_ident")
        s_factors = sem("s_factors")
        s_apart = sem("s_apart")
        s_fused = sem("s_fused")
        s_fused_kept = sem("s_fused_kept")
        s_a_exp = sem("s_a_exp")
        s_const_dve = sem("s_const_dve")
        s_const_pool = sem("s_const_pool")
        s_raw_gu = [sem(f"s_raw_gu{i}") for i in range(2)]
        s_raw_dn = [sem(f"s_raw_dn{i}") for i in range(2)]
        s_raw_copied = sem("s_raw_copied")
        s_gu_hi = sem("s_gu_hi")
        s_gu_lo = sem("s_gu_lo")
        s_dn_hi = sem("s_dn_hi")
        s_dn_lo = sem("s_dn_lo")
        s_gu_kept = [sem(f"s_gu_kept{i}") for i in range(2)]
        s_dn_kept = [sem(f"s_dn_kept{i}") for i in range(2)]
        s_x_ln = sem("s_x_ln")
        s_x_res = sem("s_x_res")
        s_wgu = [sem(f"s_wgu{i}") for i in range(2)]
        s_wdn = [sem(f"s_wdn{i}") for i in range(2)]
        s_rows = [sem(f"s_rows{i}") for i in range(2)]
        s_row_b0 = sem("s_row_b0")
        s_bc_stored = sem("s_bc_stored")
        s_w_stored = sem("s_w_stored")
        s_out = sem("s_out")
        s_filled = sem("s_filled")
        s_read = sem("s_read")
        names = """xnT_hi stats mean_var var_eps rstd xn top without_top chosen aff_e aff_d aff aff_top aff_sum
            aff_sum_eps aff_inv weight weight_hi weight_lo past_in past_out conv0 conv conv_tanh conv_sig xs2 bc_hi
            z_tanh sh_tanh sh_sig sh_down sp_abs sp_e sp_ln sp_back sp_rest sp_added sp_sum delta du2 y_init h_zero
            bias yz o_sb""".split()
        S = {n: sem("s_" + n) for n in names}
        s_b = sem("s_b")
        s_c = sem("s_c")
        s_gate = sem("s_gate")
        s_up = sem("s_up")
        s_wb = sem("s_wb")
        s_down = sem("s_down")
        s_decay = sem("s_decay")
        s_tanh = sem("s_tanh")
        s_sig = sem("s_sig")
        s_gate_in = sem("s_gate_in")
        s_u_in = sem("s_u_in")
        s_scan = sem("s_scan")
        s_hc = sem("s_hc")
        s_h_last = sem("s_h_last")
        s_silu = sem("s_silu")
        s_act_up = sem("s_act_up")
        s_hidden = sem("s_hidden")
        s_hid_hi = sem("s_hid_hi")
        s_hid_lo = sem("s_hid_lo")
        s_y = sem("s_y")

        block = ctx.enter_context(nc.Block())

        setup_loads = [
            (in_w_raw[:, :, :], io["in_wT"]), (bc_wT[:, :, :], io["bc_wT"]), (out_wT[:, :, :], io["out_wT"]),
            (shared_gu_raw, io["shared_w"][:, 0:4 * NI]), (shared_dn[:, :], io["shared_w"][:, 4 * NI:6 * NI]),
            (router_w[:, :, :], io["router_w"]), (router_b[:, :], io["router_b"]),
            (down_b[0:NE, :], io["down_b"]), (down_b[NE:2 * NE, :], io["down_b"]),
            (shared_down_b[:, :], io["shared_down_b"]),
            (conv_w[:, :, :], io["conv_w"]), (conv_b[:, :], io["conv_b"]), (dt_b[:, :], io["dt_b"]),
            (a_log, io["a_log"]), (skip_d, io["skip_d"]), (gate_b[:, :], io["gate_b"]),
            (up_b[:, :], io["up_b"]), (pick_raw, io["pick"]),
        ]
        SETUP = 16 * len(setup_loads)

        ONE = 1
        counted = [*S.values(), s_x_ln, s_x_res, *s_wgu, *s_wdn, *s_rows, s_row_b0, s_bc_stored, s_w_stored, s_out,
                   s_filled, s_read, s_b, s_c, s_gate, s_up, s_wb, s_down, s_decay, s_tanh, s_sig, s_gate_in,
                   s_u_in, s_scan, s_hc, s_h_last, s_silu, s_act_up, s_hidden, s_hid_hi, s_hid_lo, s_y]

        FILLS = {
            (1, "A"): ("post", "out_proj0"), (2, "A"): ("post", "out_proj1"), (2, "B"): ("pre", "xnT0"),
            (3, "A"): ("pre", "xnT1"), (3, "B"): ("own", "z0"),
            (4, "A"): ("pre", "x0"), (4, "B"): ("pre", "logits"),
            (5, "A"): ("pre", "x1"), (5, "B"): ("post", "tokens0"),
            (6, "A"): ("pre", "x2"), (6, "B"): ("post", "tokens1"),
            (7, "A"): ("pre", "x3"), (7, "B"): ("own", "z1"),
            (8, "A"): ("own", "shared_gate"), (8, "B"): ("own", "shared_up"),
            (9, "A"): ("pre", "bc"), (9, "B"): ("own", "z2"),
            (10, "A"): ("pre", "dt0"), (11, "A"): ("pre", "dt1"), (12, "A"): ("pre", "dt2"), (12, "B"): ("own", "z3"),
            (13, "A"): ("pre", "dt3"), (13, "B"): ("pre", "weights"),
        }
        COUNT = {kind: sum(k == kind for k, _ in FILLS.values()) for kind in ("post", "pre", "own")}

        class Chunk:

            def __init__(self, c, b, half, post, own, pre, fills_before):
                self.c, self.b, self.half = c, b, half
                once = not post and not own
                self.kinds = {k for k, on in (("post", post), ("own", own), ("pre", pre), ("once", once)) if on}
                self.fills_before = fills_before
                self.order = [name for kind, name in FILLS.values() if kind in self.kinds]

            def fill(self, name):
                return self.fills_before + self.order.index(name) + 1

            def next_place(self):
                return (self.b, 1) if self.half == 0 else (self.b + 1, 0)

            def last_place(self):
                return (self.b, 0) if self.half == 1 else (self.b - 1, 1)

        start = Chunk(-1, -1, 1, False, False, True, 0)
        ahead = COUNT["pre"]
        every = sum(COUNT.values())
        first_chunk = Chunk(0, 0, 0, False, True, True, ahead)
        ahead += COUNT["pre"] + COUNT["own"]

        def all_chunks(eng, sides, steps):
            sides(start)
            steps(first_chunk)
            apart(eng)
            with eng.Fori(0, BATCH - 1) as b:
                steps(Chunk(b * 2 + 1, b, 1, True, True, True, ahead + b * (2 * every)))
                steps(Chunk(b * 2 + 2, b + 1, 0, True, True, True, ahead + b * (2 * every) + every))
            n = CHUNKS - 1
            steps(Chunk(n, BATCH - 1, 1, True, True, False, ahead + (n - 1) * every))
            sides(Chunk(CHUNKS, BATCH, 0, True, False, False, ahead + n * every - COUNT["pre"]))

        SHARED_DOWN_STEP = 14

        def crowded(ch, s):
            kind, name = FILLS.get((s, "A"), (None, ""))
            return kind in ch.kinds and name.startswith(("dt", "out_proj")) or s == SHARED_DOWN_STEP

        def beside(table, ch, s, place):
            for kind, work in table.get((s, place), ()):
                if kind in ch.kinds:
                    work(ch)

        def alone(table):
            def run(ch):
                for s, place in sorted(table, key=lambda at: (at[0], PLACES.index(at[1]))):
                    beside(table, ch, s, place)
            return run

        PLACES = ["start", "A", "early", "down", "B", "late"]

        def apart(eng):
            eng.sem_inc(s_apart, 1)

        def x_tile(dram, place):
            b, half = place
            return dram[bass.ds(b, 1), half * T:(half + 1) * T, :].rearrange("o (t p) d -> p (o t) d", p=P)

        @block.sync
        def _(sp):
            sp.dma_start(x_ln[:, :, :], x_tile(io["x"], (0, 0))).then_inc(s_x_ln, 16)
            sp.dma_start(ident[:, :], io["ident"]).then_inc(s_ident, 16)
            sp.dma_start(x_w[:, :, :], io["x_w"]).then_inc(s_factors, 16)
            sp.dma_start(dt_wT[:, :, :], io["dt_wT"]).then_inc(s_factors, 16)
            for s in counted:
                sp.sem_inc(s, ONE)
            for dst, src in setup_loads:
                sp.dma_start(dst, src).then_inc(s_setup, 16)

            def load_gu(k, s):
                sp.dma_start(w_gu[k][:, :, :, :].bitcast(F32), gu_store[s]).then_inc(s_wgu[k], 16)

            def load_dn(k, s):
                sp.dma_start(w_dn[k][:, :, :, :].bitcast(F32), dn_store[s]).then_inc(s_wdn[k], 16)

            for at in range(0, NS, NS // 4):
                some = slice(at, at + NS // 4)
                sp.dma_start(gu_store[some, :, 1, :, :], io["w_gu"][some]).then_inc(s_raw_copied, 16)
                sp.dma_start(dn_store[some, :, 1, :, :], io["w_dn"][some]).then_inc(s_raw_copied, 16)

            def load_raw_gu(k, s):
                sp.dma_start(w_gu[k][:, 1, :, :].bitcast(F32), gu_store[s, :, 1, :, :]).then_inc(s_raw_gu[k], 16)

            def load_raw_dn(k, s):
                sp.dma_start(w_dn[k][:, 1, :, :].bitcast(F32), dn_store[s, :, 1, :, :]).then_inc(s_raw_dn[k], 16)

            def keep_gu(s):
                sp.wait_ge(s_gu_lo, s + 1)
                sp.dma_start(gu_store[s], w_gu[s % 2][:, :, :, :].bitcast(F32)).then_inc(s_gu_kept[s % 2], 16)

            def keep_dn(s):
                sp.wait_ge(s_dn_lo, s + 1)
                sp.dma_start(dn_store[s], w_dn[s % 2][:, :, :, :].bitcast(F32)).then_inc(s_dn_kept[s % 2], 16)

            sp.wait_ge(s_raw_copied, 16 * 8)
            for k in range(2):
                load_raw_gu(k, k)
                load_raw_dn(k, k)

            def load_x_res(ch):
                own = "own" in ch.kinds
                for s_over, count in ((s_read, ch.fills_before), (S["sh_down"], ch.c), (S["bias"], ch.c + own),
                                      (s_w_stored, 64 * (ch.c + own))):
                    sp.wait_ge(s_over, ONE + count)
                    apart(sp)
                sp.dma_start(x_res[:, :, :], x_tile(io["x"], ch.last_place())).then_inc(s_x_res, 16)

            def load_next_x(ch):
                nxt = ((ch.b + 1) % BATCH, ch.half)
                sp.wait_ge(s_filled, ONE + ch.fill("xnT1"))
                apart(sp)
                sp.dma_start(x_ln[:, :, :], x_tile(io["x"], nxt)).then_inc(s_x_ln, 16)

            def store_bc(ch):
                _, half = ch.next_place()
                store = row_store[half]
                if ch is not start:
                    for s_loaded, loads in ((s_rows[0], NS // 2), (s_rows[1], NS // 2), (s_row_b0, 1)):
                        sp.wait_ge(s_loaded, ONE + 16 * loads * ch.c)
                        apart(sp)
                sp.wait_ge(S["bc_hi"], ONE + ch.c + 2)
                apart(sp)
                sp.dma_start(store[:, 0, :], bc_hi[0:NS, :].bitcast(F32)).then_inc(s_bc_stored, 16)
                sp.dma_start(store[:, 2, :], bc_hi[NS:2 * NS, :].bitcast(F32)).then_inc(s_bc_stored, 16)
                sp.wait_ge(s_read, ONE + ch.fill("bc"))
                apart(sp)
                sp.dma_start(store[:, 1, :], bc_lo[0:NS, :].bitcast(F32)).then_inc(s_bc_stored, 16)
                sp.dma_start(store[:, 3, :], bc_lo[NS:2 * NS, :].bitcast(F32)).then_inc(s_bc_stored, 16)

            def load_b0(ch):
                _, half = ch.next_place()
                sp.wait_ge(s_bc_stored, ONE + 64 * (ch.c + 2))
                apart(sp)
                if ch is not start:
                    sp.wait_ge(s_b, ONE + NS * ch.c + 1)
                    apart(sp)
                sp.dma_start(row_b0[:, :].bitcast(F32), row_store[half][NS - 1, 0:2]).then_inc(s_row_b0, 16)

            def store_weights(ch):
                _, half = ch.next_place()
                sp.wait_ge(s_read, ONE + ch.fill("weights"))
                apart(sp)
                for part in range(2):
                    for e in range(EN):
                        sp.dma_start(row_store[half][:, 4 + 2 * e + part, :],
                                     weight_rows[part * NE + e * NS:part * NE + (e + 1) * NS, :])\
                          .then_inc(s_w_stored, 16)

            def store_out(ch):
                sp.wait_ge(s_read, ONE + ch.fill("tokens1"))
                apart(sp)
                sp.dma_start(x_tile(io["out"], ch.last_place()), o_tok[:, :, :]).then_inc(s_out, 16)

            def first_rows(ch):
                _, half = ch.next_place()
                sp.wait_ge(s_w_stored, ONE + 64 * (ch.c + 2))
                sp.wait_ge(s_bc_stored, ONE + 64 * (ch.c + 2))
                apart(sp)

            table = {
                (0, "late"): [("post", load_x_res)],
                (4, "late"): [("pre", load_next_x)],
                (7, "early"): [("post", store_out)],
                (9, "late"): [("pre", store_bc)],
                (10, "late"): [("pre", load_b0)],
                (14, "A"): [("pre", store_weights)],
            }

            def sides(ch):
                if ch is start:
                    load_next_x(ch)
                    store_bc(ch)
                    load_b0(ch)
                    store_weights(ch)
                    first_rows(ch)
                    for s in range(2):
                        sp.dma_start(rows[s][:, :].bitcast(F32), row_store[0][s]).then_inc(s_rows[s], 16)
                    keep_gu(0)
                else:
                    load_x_res(ch)
                    store_out(ch)

            def steps(ch):
                first = ch is first_chunk
                for s in range(NS):
                    n, k = ch.c * NS + s, s % 2
                    pre = "pre" in ch.kinds
                    beside(table, ch, s, "early")
                    if (s + 1 < NS or pre) and not (first and s == 0):
                        sp.wait_ge(s_down, ONE + EN * n)
                        apart(sp)
                        if first:
                            sp.wait_ge(s_dn_kept[1 - k], 16 * ((s - 1) // 2 + 1))
                        (load_raw_dn if first and s + 1 < NS else load_dn)(1 - k, (s + 1) % NS)
                    if s + 2 < NS or pre:
                        sp.wait_ge(s_up, ONE + EN * (n + 1))
                        apart(sp)
                        if first:
                            sp.wait_ge(s_gu_kept[k], 16 * (s // 2 + 1))
                        (load_raw_gu if first and s + 2 < NS else load_gu)(k, (s + 2) % NS)
                    beside(table, ch, s, "A")
                    if s == NS - 2 and pre:
                        first_rows(ch)
                    if s + 2 < NS or pre:
                        sp.wait_ge(s_b, ONE + n + 2)
                        sp.wait_ge(s_wb, ONE + EN * (n + 1))
                        apart(sp)
                        store = row_store[ch.half if s + 2 < NS else ch.next_place()[1]]
                        sp.dma_start(rows[k][:, :].bitcast(F32), store[(s + 2) % NS]).then_inc(s_rows[k], 16)
                    if first and s + 1 < NS:
                        keep_gu(s + 1)
                    if first:
                        keep_dn(s)
                    if first and s == NS - 1:
                        sp.wait_ge(s_dn_kept[k], 16 * (NS // 2))
                    beside(table, ch, s, "late")

            all_chunks(sp, sides, steps)
            sp.wait_ge(s_out, ONE + 16 * CHUNKS)

        @block.gpsimd
        def _(pool):
            pool.memset(minus_half[:, :], -0.5).then_inc(s_const_pool, 1)
            pool.wait_ge(s_const_pool, 1)
            pool.memset(ones_row[:, :], 1.0).then_inc(s_const_pool, 1)
            pool.wait_ge(s_const_pool, 2)
            pool.memset(no_past[:, :, :], 0.0).then_inc(s_const_pool, 1)
            pool.wait_ge(s_const_pool, 3)

            def make_rstd(ch):
                n = ch.c + 1
                pool.wait_ge(S["mean_var"], ONE + TT * (n + 1))
                pool.wait_ge(S["rstd"], ONE + n)
                apart(pool)
                pool.tensor_scalar(var_eps[:, :], mean_var[:, :, 1], LN_EPS, None, ALU.add).then_inc(S["var_eps"], 1)
                pool.wait_ge(S["var_eps"], ONE + n + 1)
                pool.wait_ge(S["xn"], ONE + TT * n)
                pool.tensor_tensor(rstd[:, :], var_eps[:, :], minus_half[:, :], ALU.pow).then_inc(S["rstd"], 1)

            def gate_x(g):
                def work(ch):
                    n = ch.c + 1
                    pool.wait_ge(S["conv_sig"], ONE + G * n + g + 1)
                    pool.wait_ge(S["y_init"], ONE + G * n)
                    pool.wait_ge(S["du2"], ONE + n)
                    pool.wait_ge(s_filled, ONE + ch.fills_before)
                    pool.tensor_tensor(xs2[:, g, :], conv_tanh[g % 2], conv[g % 2], ALU.mult).then_inc(S["xs2"], 1)
                return work

            def softplus_rest(g):
                def work(ch):
                    pool.wait_ge(S["sp_back"], ONE + G * (ch.c + 1) + g + 1)
                    pool.tensor_tensor(sp_back[:, g, :], sp_e[:, g, :], sp_back[:, g, :], ALU.subtract)\
                        .then_inc(S["sp_rest"], 1)
                    if g < G - 1:
                        tile = delta[ch.next_place()[1]][:, g, :]
                        pool.wait_ge(s_read, ONE + ch.fill(f"dt{g}"))
                        pool.wait_ge(S["sp_rest"], ONE + G * (ch.c + 1) + g + 1)
                        pool.tensor_tensor(tile, tile, sp_back[:, g, :], ALU.add).then_inc(S["sp_added"], 1)
                return work

            table = {
                (1, "late"): [("pre", make_rstd)],
                **{(5 + g, "early"): [("pre", gate_x(g))] for g in range(G)},
                **{(12 + g, "early"): [("pre", softplus_rest(g))] for g in range(G)},
            }

            def split_low(tile, s, s_hi, s_lo):
                pool.wait_ge(s_hi, s + 1)
                pool.tensor_tensor(tile[:, 1, :, :], tile[:, 1, :, :].bitcast(F32), tile[:, 0, :, :].bitcast(F32),
                                   ALU.subtract).then_inc(s_lo, 1)

            def gu_low(s):
                split_low(w_gu[s % 2], s, s_gu_hi, s_gu_lo)

            def dn_low(s):
                split_low(w_dn[s % 2], s, s_dn_hi, s_dn_lo)

            def steps(ch):
                for s in range(NS):
                    def add_y(n, part):
                        pool.wait_ge(s_hc, ONE + n + 1)
                        pool.wait_ge(s_y, ONE + 2 * n + part)
                        blocks = slice(2 * part, 2 * part + 2)
                        pool.tensor_tensor(y[:, blocks, :], y[:, blocks, :], hc[:, blocks, :], ALU.add)\
                            .then_inc(s_y, 1)

                    def silu(n, j):
                        pool.wait_ge(s_sig, ONE + EN * n + j + 1)
                        pool.tensor_tensor(act_tile[j][:, :], act_tile[j][:, :], gate_in[j][:, :], ALU.mult)\
                            .then_inc(s_silu, 1)

                    def low(n, j):
                        pool.wait_ge(s_hid_hi, ONE + EN * n + j + 1)
                        pool.tensor_tensor(hid_lo[j][:, :], act_tile[j][:, :], hid_hi[j][:, :].bitcast(F32),
                                           ALU.subtract).then_inc(s_hid_lo, 1)

                    n = ch.c * NS + s
                    very_first = ch is first_chunk and s == 0
                    if very_first:
                        silu(n, 0)
                    if s == 1:
                        pool.wait_ge(S["y_init"], ONE + G * (ch.c + 1))
                        apart(pool)
                    if not very_first:
                        add_y(n - 1, 0)
                        low(n - 1, 1)
                        silu(n, 0)
                        add_y(n - 1, 1)
                    if ch is first_chunk and s + 1 < NS:
                        gu_low(s + 1)
                    beside(table, ch, s, "early")
                    silu(n, 1)
                    low(n, 0)
                    if ch is first_chunk:
                        dn_low(s)
                    if s == NS - 1 and "pre" not in ch.kinds:
                        low(n, 1)
                        add_y(n, 0)
                        add_y(n, 1)
                    beside(table, ch, s, "late")

            table[(14, "early")].append(("once", lambda _: gu_low(0)))
            all_chunks(pool, alone(table), steps)

        @block.scalar
        def _(act):
            def constants(_):
                act.wait_ge(s_setup, SETUP)
                act.activation(a_exp, a_log, ACT.Exp).then_inc(s_a_exp, 1)

            def take_out(ch):
                act.wait_ge(s_down, ONE + NE * ch.c)
                act.wait_ge(S["sh_down"], ONE + ch.c)
                act.wait_ge(s_read, ONE + ch.fills_before)
                act.wait_ge(S["delta"], ONE + ch.c + ("own" in ch.kinds))
                for m in range(KM):
                    act.activation(o_sb[:, m, :], p_out[m][:, :], ACT.Identity,
                                   bias=shared_down_b[:, m:m + 1]).then_inc(S["o_sb"], 1)

            def y_init(ch):
                act.wait_ge(S["yz"], ONE + G * ch.c)
                for g in range(G):
                    act.activation(y[:, g, :], xs2[:, g, :], ACT.Copy, scale=half_d[:, g:g + 1])\
                       .then_inc(S["y_init"], 1)

            def take_xnT(k):
                def work(ch):
                    act.wait_ge(s_up, ONE + NE * ch.c if ch is not start else ONE)
                    act.wait_ge(s_filled, ONE + ch.fill(f"xnT{k}"))
                    act.activation(xnT[ch.next_place()[1]][:, 0, k, :], p_side[:, :], ACT.Copy).then_inc(S["xnT_hi"], 1)
                return work

            def take_x(g):
                def work(ch):
                    n, (_, half), tile = ch.c + 1, ch.next_place(), x_pad[g % 2]
                    act.wait_ge(s_bc_stored, ONE + 64 * n)
                    act.wait_ge(S["conv"], ONE + (TAPS - 1) * (G * n + g - 1) if g > 1 else ONE + (TAPS - 1) * G * n)
                    source = no_past if half == 0 else past
                    act.wait_ge(S["past_out"], ONE + G * n + g)
                    act.activation(tile[:, 0:PAD], source[:, g, :], ACT.Copy).then_inc(S["past_in"], 1)
                    act.wait_ge(s_filled, ONE + ch.fill(f"x{g}"))
                    act.activation(tile[:, PAD:PAD + T], p_side[:, :], ACT.Copy).then_inc(s_read, 1)
                    act.wait_ge(s_read, ONE + ch.fill(f"x{g}"))
                    act.wait_ge(S["past_in"], ONE + G * n + g + 1)
                    act.wait_ge(S["xs2"], ONE + G * n + max(g - 1, 0))
                    act.wait_ge(S["sp_sum"], ONE + n)
                    act.activation(conv[g % 2], tile[:, 0:T], ACT.Identity, scale=conv_w[:, g, 0:1],
                                   bias=conv_b[:, g:g + 1]).then_inc(S["conv0"], 1)
                    act.activation(past[:, g, :], tile[:, T:T + PAD], ACT.Copy).then_inc(S["past_out"], 1)
                return work

            def tanh_conv(g):
                def work(ch):
                    n = ch.c + 1
                    act.wait_ge(S["conv"], ONE + (TAPS - 1) * (G * n + g + 1))
                    act.wait_ge(S["xs2"], ONE + G * n + max(g - 1, 0))
                    act.activation(conv_tanh[g % 2], conv[g % 2], ACT.Tanh, scale=0.5).then_inc(S["conv_tanh"], 1)
                    act.wait_ge(S["conv_tanh"], ONE + G * n + g + 1)
                    act.activation(conv_tanh[g % 2], conv_tanh[g % 2], ACT.Identity, bias=1.0)\
                       .then_inc(S["conv_sig"], 1)
                return work

            def tanh_z(g):
                def work(ch):
                    act.wait_ge(s_filled, ONE + ch.fill(f"z{g}"))
                    act.wait_ge(s_read, ONE + ch.fill(f"z{g}") - 1)
                    act.activation(z_tanh[:, :], p_side[:, :], ACT.Tanh, scale=0.5).then_inc(S["z_tanh"], 1)
                return work

            def shared_tanh(ch):
                act.wait_ge(s_filled, ONE + ch.fill("shared_gate"))
                act.wait_ge(s_read, ONE + ch.fill("shared_gate") - 1)
                act.activation(shared_sig[:, :], p_side[:, :], ACT.Tanh, scale=0.5,
                               bias=half_gate_b[:, NE:NE + 1]).then_inc(S["sh_tanh"], 1)
                act.wait_ge(S["sh_tanh"], ONE + ch.c + 1)
                act.activation(shared_sig[:, :], shared_sig[:, :], ACT.Identity, bias=1.0).then_inc(S["sh_sig"], 1)

            def router_exp(ch):
                n = ch.c + 1
                act.wait_ge(s_read, ONE + ch.fill("logits"))
                act.wait_ge(S["aff"], ONE + n)
                act.activation(aff_e[:, :, :], logits[:, :, :], ACT.Exp, scale=-1.0).then_inc(S["aff_e"], 1)

            def take_dt(g):
                def work(ch):
                    n, (_, half) = ch.c + 1, ch.next_place()
                    act.wait_ge(s_filled, ONE + ch.fill(f"dt{g}"))
                    if g == 0:
                        act.wait_ge(S["delta"], ONE + n)
                    act.activation(sp_e[:, g, :], p_side[:, :], ACT.Abs, bias=dt_b[:, g:g + 1])\
                       .then_inc(S["sp_abs"], 1)
                    act.activation(delta[half][:, g, :], p_side[:, :], ACT.Relu, bias=dt_b[:, g:g + 1])\
                       .then_inc(s_read, 1)
                return work

            def softplus_exp(g):
                def work(ch):
                    n = ch.c + 1
                    act.wait_ge(S["sp_abs"], ONE + G * n + g + 1)
                    act.activation(sp_e[:, g, :], sp_e[:, g, :], ACT.Exp, scale=-1.0).then_inc(S["sp_e"], 1)
                return work

            def softplus_ln(ch):
                n = ch.c + 1
                act.wait_ge(S["xs2"], ONE + G * (n + 1))
                act.wait_ge(S["sp_e"], ONE + G * (n + 1))
                act.activation(sp_ln[:, :, :], sp_e[:, :, :], ACT.Ln, bias=1.0).then_inc(S["sp_ln"], 1)
                act.preload_act_table(ACT.Tanh)

            def take_weights(ch):
                n = ch.c + 1
                act.wait_ge(s_filled, ONE + ch.fill("weights"))
                act.wait_ge(s_w_stored, ONE + 64 * n)
                act.wait_ge(S["bias"], ONE + n)
                act.activation(weight_rows, p_side[0:2 * NE, :], ACT.Copy).then_inc(s_read, 1)

            table = {
                (0, "early"): [("post", take_out)],
                (0, "late"): [("own", y_init)],
                (3, "start"): [("pre", take_xnT(0))], (3, "late"): [("pre", take_xnT(1)), ("once", constants)],
                (4, "start"): [("own", tanh_z(0))], (4, "late"): [("pre", take_x(0))],
                (5, "start"): [("pre", tanh_conv(0))], (5, "late"): [("pre", take_x(1)), ("pre", router_exp)],
                (6, "start"): [("pre", tanh_conv(1))], (6, "late"): [("pre", take_x(2))],
                (7, "start"): [("pre", tanh_conv(2))], (7, "late"): [("pre", take_x(3))],
                (8, "start"): [("own", tanh_z(1)), ("pre", tanh_conv(3))], (8, "late"): [("own", shared_tanh)],
                (10, "start"): [("own", tanh_z(2))], (10, "late"): [("pre", take_dt(0))],
                (11, "start"): [("pre", softplus_exp(0))], (11, "late"): [("pre", take_dt(1))],
                (12, "start"): [("pre", softplus_exp(1))], (12, "late"): [("pre", take_dt(2))],
                (13, "start"): [("own", tanh_z(3)), ("pre", softplus_exp(2))], (13, "late"): [("pre", take_dt(3))],
                (14, "start"): [("pre", softplus_exp(3)), ("pre", take_weights)],
                (14, "late"): [("pre", softplus_ln)],
            }

            def gu_high(s):
                tile = w_gu[s % 2]
                act.wait_ge(s_raw_gu[s % 2], 16 * (s // 2 + 1))
                act.activation(tile[:, 0, :, :], tile[:, 1, :, :].bitcast(F32), ACT.Copy).then_inc(s_gu_hi, 1)

            def dn_high(s):
                tile = w_dn[s % 2]
                act.wait_ge(s_raw_dn[s % 2], 16 * (s // 2 + 1))
                act.activation(tile[:, 0, :, :], tile[:, 1, :, :].bitcast(F32), ACT.Copy).then_inc(s_dn_hi, 1)

            def steps(ch):
                for s in range(NS):
                    n = ch.c * NS + s

                    def decay(n, s, g):
                        act.wait_ge(s_scan, ONE + G * n + g)
                        act.activation(p_decay[:, :], delta[ch.half][:, g, :], ACT.Exp,
                                       scale=a_neg[:, s * G + g:s * G + g + 1]).then_inc(s_decay, 1)

                    def gate(n, s, j):
                        act.wait_ge(s_gate, ONE + EN * n + j + 1)
                        if not (ch is first_chunk and n == 0):
                            act.wait_ge(s_hid_lo, ONE + EN * (n - 1) + j + 1)
                        act.activation(act_tile[j][:, :], p_gate[:, :], ACT.Tanh, scale=0.5,
                                       bias=half_gate_b[:, s * EN + j:s * EN + j + 1]).then_inc(s_tanh, 1)
                        act.activation(gate_in[j][:, :], p_gate[:, :], ACT.Identity,
                                       bias=gate_b[:, s * EN + j:s * EN + j + 1]).then_inc(s_gate_in, 1)

                    def sig(n, j):
                        act.wait_ge(s_tanh, ONE + EN * n + j + 1)
                        act.activation(act_tile[j][:, :], act_tile[j][:, :], ACT.Identity, bias=1.0)\
                           .then_inc(s_sig, 1)

                    def high(n, j):
                        act.wait_ge(s_hidden, ONE + EN * n + j + 1)
                        if not (ch is first_chunk and n == 0):
                            act.wait_ge(s_down, ONE + EN * (n - 1) + j + 1)
                        act.activation(hid_hi[j][:, :], act_tile[j][:, :], ACT.Copy).then_inc(s_hid_hi, 1)

                    very_first = ch is first_chunk and s == 0
                    if very_first:
                        gate(n, s, 0)
                        sig(n, 0)
                    if s == 0:
                        act.wait_ge(S["delta"], ONE + ch.c + 1)
                        decay(n, s, 0)
                    if s == 0 and not very_first:
                        high(n - 1, 1)
                    decay(n, s, 1)
                    if ch is first_chunk:
                        if s + 1 < NS:
                            gu_high(s + 1)
                        dn_high(s)
                    beside(table, ch, s, "start")
                    decay(n, s, 2)
                    if s < NS - 1:
                        gate(n, s, 1)
                    decay(n, s, 3)
                    if s == NS - 1:
                        gate(n, s, 1)
                    sig(n, 1)
                    high(n, 0)
                    beside(table, ch, s, "early")
                    act.wait_ge(s_scan, ONE + G * (n + 1))
                    act.activation(h_last[:, s, :], h[:, :, T - 1], ACT.Copy).then_inc(s_h_last, 1)
                    if s < NS - 1:
                        decay(n + 1, s + 1, 0)
                    beside(table, ch, s, "late")
                    ahead_first = s < NS - 1 and not crowded(ch, s)
                    if s < NS - 1 and not ahead_first or "pre" not in ch.kinds and s == NS - 1:
                        high(n, 1)
                    if s < NS - 1 or "pre" in ch.kinds:
                        gate(n + 1, (s + 1) % NS, 0)
                        sig(n + 1, 0)
                    if ahead_first:
                        high(n, 1)

            table[(12, "late")].append(("once", lambda _: gu_high(0)))
            all_chunks(act, alone(table), steps)

        @block.vector
        def _(dve):
            def constants(_):
                dve.wait_ge(s_setup, SETUP)
                consts = [
                    dve.tensor_copy(pick[:, :, :], pick_raw),
                    dve.tensor_scalar(half_gate_b[:, :], gate_b[:, :], 0.5, None, ALU.mult),
                    dve.tensor_scalar(half_d[:, :], skip_d, 0.5, None, ALU.mult),
                    dve.tensor_scalar(bc_wT[:, :, 0:NS], bc_wT[:, :, 0:NS], 0.25, None, ALU.mult),
                    dve.tensor_scalar(bc_wT[:, :, NS:2 * NS], bc_wT[:, :, NS:2 * NS], 0.5, None, ALU.mult),
                    dve.tensor_scalar(shared_dn[:, :], shared_dn[:, :], 0.5, None, ALU.mult),
                    dve.tensor_copy(in_w[:, 0, :, :], in_w_raw[:, :, :]),
                    dve.tensor_copy(shared_gu[:, 0, :], shared_gu_raw),
                ]
                for made in consts:
                    made.then_inc(s_const_dve, 1)
                dve.wait_ge(s_a_exp, 1)
                dve.tensor_scalar(a_neg[:, :], a_exp, -1.0, None, ALU.mult).then_inc(s_const_dve, 1)
                dve.wait_ge(s_const_dve, len(consts))
                dve.tensor_tensor(in_w[:, 1, :, :], in_w_raw[:, :, :], in_w[:, 0, :, :].bitcast(F32),
                                  ALU.subtract).then_inc(s_const_dve, 1)
                dve.tensor_tensor(shared_gu[:, 1, :], shared_gu_raw, shared_gu[:, 0, :].bitcast(F32),
                                  ALU.subtract).then_inc(s_const_dve, 1)

            def keep_fused(_):
                for g in range(G):
                    dve.wait_ge(s_fused, g + 1)
                    dve.tensor_scalar(dt_fused[:, g, :], fused_banks[g][:, :], 0.5, None, ALU.mult)\
                       .then_inc(s_fused_kept, 1)

            def yz(ch):
                dve.wait_ge(s_y, ONE + 2 * NS * ch.c)
                dve.wait_ge(s_read, ONE + ch.fills_before)
                for g in range(G):
                    dve.scalar_tensor_tensor(out=z_gate[:, g, :], in0=y[:, g, :], scalar=0.5, in1=z_gate[:, g, :],
                                             op0=ALU.mult, op1=ALU.mult).then_inc(S["yz"], 1)

            def norm_stats(ch):
                n = ch.c + 1
                dve.wait_ge(s_x_ln, ONE + 16 * (n + 1))
                dve.wait_ge(S["mean_var"], ONE + TT * n)
                apart(dve)
                for t in range(TT):
                    dve.bn_stats(stats[:, t, :], x_ln[:, t, :]).then_inc(S["stats"], 1)

            def norm_aggr(ch):
                n = ch.c + 1
                dve.wait_ge(S["var_eps"], ONE + n)
                dve.wait_ge(S["xn"], ONE + TT * n)
                dve.wait_ge(S["stats"], ONE + TT * (n + 1))
                apart(dve)
                for t in range(TT):
                    dve.bn_aggr(mean_var[:, t, :], stats[:, t, :]).then_inc(S["mean_var"], 1)

            def norm(ch):
                n = ch.c + 1
                dve.wait_ge(S["rstd"], ONE + n + 1)
                dve.wait_ge(S["mean_var"], ONE + TT * (n + 1))
                for t in range(TT):
                    dve.tensor_scalar(x_ln[:, t, :], x_ln[:, t, :], mean_var[:, t, 0:1], rstd[:, t:t + 1],
                                      ALU.subtract, ALU.mult).then_inc(S["xn"], 1)

            def low_x(k):
                def work(ch):
                    tile = xnT[ch.next_place()[1]]
                    dve.wait_ge(S["xnT_hi"], ONE + KM * (ch.c + 1) + k + 1)
                    dve.tensor_tensor(tile[:, 1, k, :], p_side[:, :], tile[:, 0, k, :].bitcast(F32), ALU.subtract)\
                       .then_inc(s_read, 1)
                return work

            def add_out(m):
                def work(ch):
                    dve.wait_ge(s_filled, ONE + ch.fill(f"out_proj{m}"))
                    dve.wait_ge(S["o_sb"], ONE + KM * (ch.c - 1) + m + 1)
                    dve.tensor_tensor(o_sb[:, m, :], p_side[:, :], o_sb[:, m, :], ALU.add).then_inc(s_read, 1)
                return work

            def add_residual(q):
                def work(ch):
                    dve.wait_ge(s_filled, ONE + ch.fill(f"tokens{q}"))
                    dve.wait_ge(s_x_res, ONE + 16 * ch.c)
                    dve.wait_ge(s_out, ONE + 16 * (ch.c - 1))
                    dve.tensor_tensor(o_tok[:, 2 * q:2 * q + 2, :],
                                      p_side[:, :].rearrange("p (t d) -> p t d", d=DM),
                                      x_res[:, 2 * q:2 * q + 2, :], ALU.add).then_inc(s_read, 1)
                return work

            def gate_z(g):
                def work(ch):
                    dve.wait_ge(S["z_tanh"], ONE + G * ch.c + g + 1)
                    dve.wait_ge(s_filled, ONE + ch.fill(f"z{g}"))
                    dve.scalar_tensor_tensor(out=z_gate[:, g, :], in0=z_tanh[:, :], scalar=1.0, in1=p_side[:, :],
                                             op0=ALU.add, op1=ALU.mult).then_inc(s_read, 1)
                return work

            def take_logits(ch):
                n = ch.c + 1
                dve.wait_ge(s_filled, ONE + ch.fill("logits"))
                dve.wait_ge(S["aff_e"], ONE + n)
                dve.wait_ge(S["chosen"], ONE + n)
                dve.tensor_copy(logits[:, :, :], p_side[:, 0:TT * NE].rearrange("p (t e) -> p t e", e=NE))\
                   .then_inc(s_read, 1)

            def convolve(g):
                def work(ch):
                    n, tile = ch.c + 1, x_pad[g % 2]
                    dve.wait_ge(s_read, ONE + ch.fill(f"x{g}"))
                    dve.wait_ge(S["conv0"], ONE + G * n + g + 1)
                    for tap in range(1, TAPS):
                        dve.wait_ge(S["conv"], ONE + (TAPS - 1) * (G * n + g) + tap - 1)
                        dve.scalar_tensor_tensor(out=conv[g % 2], in0=tile[:, tap:tap + T],
                                                 scalar=conv_w[:, g, tap:tap + 1], in1=conv[g % 2],
                                                 op0=ALU.mult, op1=ALU.add).then_inc(S["conv"], 1)
                return work

            def find_top(ch):
                n = ch.c + 1
                dve.wait_ge(s_read, ONE + ch.fill("logits"))
                dve.wait_ge(S["without_top"], ONE + TT * n)
                apart(dve)
                for t in range(TT):
                    dve.max(top[:, t, :], logits[:, t, :]).then_inc(S["top"], 1)

            def take_top(ch):
                n = ch.c + 1
                dve.wait_ge(S["top"], ONE + TT * (n + 1))
                dve.wait_ge(S["chosen"], ONE + n)
                apart(dve)
                for t in range(TT):
                    dve.match_replace(without_top[:, t, :], in_to_replace=top[:, t, :], in_values=logits[:, t, :],
                                      imm_value=BELOW_ALL).then_inc(S["without_top"], 1)

            def sigmoid(ch):
                n = ch.c + 1
                dve.wait_ge(S["aff_e"], ONE + n + 1)
                dve.tensor_scalar(aff_e[:, :, :], aff_e[:, :, :], 1.0, None, ALU.add).then_inc(S["aff_d"], 1)
                dve.wait_ge(S["without_top"], ONE + TT * (n + 1))
                dve.wait_ge(S["aff_top"], ONE + n)
                dve.tensor_tensor(chosen[:, :, :], without_top[:, :, :], logits[:, :, :], ALU.not_equal)\
                   .then_inc(S["chosen"], 1)
                dve.wait_ge(S["aff_d"], ONE + n + 1)
                dve.reciprocal(aff[:, :, :], aff_e[:, :, :]).then_inc(S["aff"], 1)

            def sum_top(ch):
                n = ch.c + 1
                dve.wait_ge(S["aff"], ONE + n + 1)
                dve.wait_ge(S["chosen"], ONE + n + 1)
                dve.wait_ge(S["weight_lo"], ONE + n)
                dve.tensor_tensor(aff_top[:, :, :], aff[:, :, :], chosen[:, :, :], ALU.mult).then_inc(S["aff_top"], 1)
                dve.wait_ge(S["aff_top"], ONE + n + 1)
                dve.tensor_reduce(aff_sum[:, :], aff_top[:, :, :], AX.X, ALU.add).then_inc(S["aff_sum"], 1)

            def invert_sum(ch):
                n = ch.c + 1
                dve.wait_ge(S["aff_sum"], ONE + n + 1)
                dve.tensor_scalar(aff_sum[:, :], aff_sum[:, :], SUM_EPS, None, ALU.add).then_inc(S["aff_sum_eps"], 1)
                dve.wait_ge(S["aff_sum_eps"], ONE + n + 1)
                dve.reciprocal(aff_inv[:, :], aff_sum[:, :]).then_inc(S["aff_inv"], 1)

            def weigh(ch):
                n = ch.c + 1
                dve.wait_ge(S["aff_inv"], ONE + n + 1)
                dve.wait_ge(S["weight_lo"], ONE + n)
                dve.tensor_tensor(aff_top[:, :, :], aff_top[:, :, :],
                                  aff_inv[:, :].rearrange("p (t o) -> p t o", o=1).broadcast_to([P, TT, NE]),
                                  ALU.mult).then_inc(S["weight"], 1)

            def split_weights(ch):
                n = ch.c + 1
                dve.wait_ge(S["weight"], ONE + n + 1)
                dve.wait_ge(s_filled, ONE + ch.fills_before)
                dve.tensor_copy(weight_split[:, :, 0, :], aff_top[:, :, :]).then_inc(S["weight_hi"], 1)
                dve.wait_ge(S["weight_hi"], ONE + n + 1)
                dve.tensor_tensor(weight_split[:, :, 1, :], aff_top[:, :, :], weight_split[:, :, 0, :].bitcast(F32),
                                  ALU.subtract).then_inc(S["weight_lo"], 1)

            def shared_silu(ch):
                dve.wait_ge(S["sh_sig"], ONE + ch.c + 1)
                dve.wait_ge(S["sh_down"], ONE + ch.c)
                dve.scalar_tensor_tensor(out=shared_sig[:, :], in0=p_side[:, :], scalar=gate_b[:, NE:NE + 1],
                                         in1=shared_sig[:, :], op0=ALU.add, op1=ALU.mult).then_inc(s_read, 1)

            def shared_times_up(ch):
                dve.wait_ge(s_filled, ONE + ch.fill("shared_up"))
                dve.wait_ge(s_read, ONE + ch.fill("shared_gate"))
                dve.scalar_tensor_tensor(out=shared_up, in0=p_side[:, :], scalar=up_b[:, NE:NE + 1],
                                         in1=shared_sig[:, :], op0=ALU.add, op1=ALU.mult).then_inc(s_read, 1)

            def split_bc(ch):
                n = ch.c + 1
                dve.wait_ge(s_filled, ONE + ch.fill("bc"))
                dve.wait_ge(S["past_out"], ONE + G * (n + 1))
                dve.wait_ge(S["conv"], ONE + (TAPS - 1) * G * (n + 1))
                dve.tensor_copy(bc_hi[:, :], p_side[0:2 * NS, :]).then_inc(S["bc_hi"], 1)
                dve.wait_ge(S["bc_hi"], ONE + n + 1)
                dve.tensor_tensor(bc_lo[:, :], p_side[0:2 * NS, :], bc_hi[:, :].bitcast(F32), ALU.subtract)\
                   .then_inc(s_read, 1)

            def softplus_back(g):
                def work(ch):
                    n = ch.c + 1
                    if g == 0 and ch is not start:
                        dve.wait_ge(s_out, ONE + 16 * ch.c)
                        dve.wait_ge(S["delta"], ONE + n)
                    dve.wait_ge(S["sp_e"], ONE + G * n + g + 1)
                    dve.tensor_scalar(sp_back[:, g, :], sp_e[:, g, :], 1.0, 1.0, ALU.add, ALU.subtract)\
                       .then_inc(S["sp_back"], 1)
                return work

            def add_rest(ch):
                n, (_, half), g = ch.c + 1, ch.next_place(), G - 1
                dve.wait_ge(S["sp_rest"], ONE + G * (n + 1))
                dve.wait_ge(S["sp_sum"], ONE + n + 1)
                dve.tensor_tensor(delta[half][:, g, :], delta[half][:, g, :], sp_back[:, g, :], ALU.add)\
                   .then_inc(S["delta"], 1)

            def softplus_sum(ch):
                n, (_, half) = ch.c + 1, ch.next_place()
                dve.wait_ge(S["sp_ln"], ONE + n + 1)
                dve.wait_ge(S["sp_added"], ONE + (G - 1) * (n + 1))
                dve.wait_ge(s_read, ONE + ch.fill("dt3"))
                dve.tensor_tensor(delta[half][:, :, :], delta[half][:, :, :], sp_ln[:, :, :], ALU.add)\
                   .then_inc(S["sp_sum"], 1)

            def delta_x(ch):
                n, (_, half) = ch.c + 1, ch.next_place()
                dve.wait_ge(S["delta"], ONE + n + 1)
                dve.wait_ge(S["xs2"], ONE + G * (n + 1))
                if ch is not start:
                    dve.wait_ge(s_u_in, ONE + 2 * NS * n)
                dve.tensor_tensor(du2[:, :, :], delta[half][:, :, :], xs2[:, :, :], ALU.mult)\
                   .then_inc(S["du2"], 1)

            table = {
                (0, "early"): [("post", yz)], (0, "late"): [("pre", norm_stats)],
                (1, "start"): [("pre", norm_aggr)], (1, "late"): [("post", add_out(0))],
                (2, "start"): [("pre", norm)], 
                (2, "late"): [("post", add_out(1))],
                (3, "start"): [("pre", low_x(0))], (3, "late"): [("pre", low_x(1)), ("once", constants)],
                (4, "start"): [("own", gate_z(0))], (4, "late"): [("pre", convolve(0))],
                (5, "start"): [("pre", take_logits)], (5, "late"): [("once", keep_fused), ("pre", convolve(1))],
                (6, "start"): [("post", add_residual(0))],
                (6, "late"): [("pre", find_top), ("pre", convolve(2))],
                (7, "start"): [("post", add_residual(1))],
                (7, "late"): [("pre", take_top), ("pre", convolve(3))],
                (8, "start"): [("own", gate_z(1))],
                (8, "late"): [("own", shared_silu), ("pre", sigmoid)],
                (9, "start"): [("own", shared_times_up), ("pre", sum_top)], (9, "late"): [("pre", split_bc)],
                (10, "start"): [("own", gate_z(2)), ("pre", invert_sum)], (10, "late"): [("pre", weigh)],
                (11, "start"): [("pre", split_weights)],
                (11, "early"): [("pre", softplus_back(0))],
                (12, "early"): [("pre", softplus_back(1))],
                (13, "early"): [("pre", softplus_back(2))],
                (14, "early"): [("pre", softplus_back(3))],
                (13, "start"): [("own", gate_z(3))],
                (15, "start"): [("pre", softplus_sum)],
                (15, "early"): [("pre", add_rest), ("pre", delta_x)],
            }

            def steps(ch):
                if ch.half == 0:
                    dve.wait_ge(s_h_last, ONE + NS * ch.c)
                    apart(dve)
                    dve.memset(h_last[:, :, :], 0.0).then_inc(S["h_zero"], 1)
                dve.wait_ge(S["h_zero"], ONE + ch.b + 1)
                dve.wait_ge(S["du2"], ONE + ch.c + 1)
                for s in range(NS):
                    n = ch.c * NS + s

                    def all_blocks(psum, blocks=G):
                        return psum[:, :].rearrange("p (o t) -> p o t", o=1).broadcast_to([P, blocks, T])

                    def scan(g):
                        dve.wait_ge(s_decay, ONE + G * n + g + 1)
                        dve.tensor_tensor_scan(h[:, g, :], p_decay[:, :], u_in[:, g, :], h_last[:, s, g:g + 1],
                                               ALU.mult, ALU.add).then_inc(s_scan, 1)

                    def times_up(j):
                        dve.wait_ge(s_up, ONE + EN * n + j + 1)
                        dve.wait_ge(s_silu, ONE + EN * n + j + 1)
                        dve.scalar_tensor_tensor(out=act_tile[j][:, :], in0=p_up[:, :],
                                                 scalar=up_b[:, s * EN + j:s * EN + j + 1], in1=act_tile[j][:, :],
                                                 op0=ALU.add, op1=ALU.mult).then_inc(s_act_up, 1)

                    def times_weight(j):
                        dve.wait_ge(s_wb, ONE + EN * n + j + 1)
                        dve.wait_ge(s_act_up, ONE + EN * n + j + 1)
                        dve.scalar_tensor_tensor(out=act_tile[j][:, :], in0=act_tile[j][:, :], scalar=0.5,
                                                 in1=p_w[:, :], op0=ALU.mult, op1=ALU.mult).then_inc(s_hidden, 1)

                    def inputs(part):
                        blocks = slice(2 * part, 2 * part + 2)
                        dve.tensor_tensor(u_in[:, blocks, :], du2[:, blocks, :], all_blocks(p_bc, 2), ALU.mult)\
                           .then_inc(s_u_in, 1)

                    dve.wait_ge(s_b, ONE + n + 1)
                    dve.wait_ge(s_hc, ONE + n)
                    dve.wait_ge(s_h_last, ONE + n)
                    inputs(0)
                    dve.wait_ge(s_u_in, ONE + 2 * n + 1)
                    scan(0)
                    inputs(1)
                    scan(1)
                    dve.wait_ge(s_u_in, ONE + 2 * n + 2)
                    times_up(0)
                    beside(table, ch, s, "start")
                    scan(2)
                    times_weight(0)
                    scan(3)
                    beside(table, ch, s, "early")
                    dve.wait_ge(s_scan, ONE + G * (n + 1))
                    dve.wait_ge(s_c, ONE + n + 1)
                    dve.wait_ge(s_y, ONE + 2 * n)
                    dve.tensor_tensor(hc[:, :, :], h[:, :, :], all_blocks(p_bc), ALU.mult).then_inc(s_hc, 1)
                    times_up(1)
                    times_weight(1)
                    beside(table, ch, s, "late")

            all_chunks(dve, alone(table), steps)

        @block.tensor
        def _(pe):
            pe.wait_ge(s_ident, 16)

            def constants(_):
                pe.wait_ge(s_setup, SETUP)
                pe.wait_ge(s_const_dve, 11)
                pe.wait_ge(s_const_pool, 3)

            def fuse(_):
                pe.wait_ge(s_factors, 32)
                for g in range(G):
                    for j in range(G):
                        mm = pe.matmul(fused_banks[g][:, :], x_w[:, j, g * P:(g + 1) * P], dt_wT[:, j, :],
                                       start=(j == 0), stop=(j == G - 1))
                    mm.then_inc(s_fused, 1)

            def fused(_):
                pe.wait_ge(s_fused_kept, G)

            def in_parts(out, factors, start=True, stop=True):
                passes = [(w[:, i], x[:, j]) for w, x in factors for i, j in ((0, 0), (0, 1), (1, 0))]
                for at, (w, x) in enumerate(passes):
                    mm = pe.matmul(out[:, :], w, x, start=(start and at == 0),
                                   stop=(stop and at == len(passes) - 1))
                return mm

            def fill(name, product):
                def work(ch):
                    pe.wait_ge(s_read, ONE + ch.fill(name) - 1)
                    product(ch).then_inc(s_filled, 1)
                return work

            def biases(ch):
                pe.wait_ge(s_read, ONE + ch.fills_before)
                pe.wait_ge(S["o_sb"], ONE + KM * ch.c)
                for m in range(KM):
                    mm = pe.matmul(p_out[m][:, :], down_b[:, m * P:(m + 1) * P], weight_rows,
                                   start=True, stop=False)
                mm.then_inc(S["bias"], 1)

            def shared_down(ch):
                pe.wait_ge(s_read, ONE + ch.fill("shared_up"))
                for m in range(KM):
                    mm = pe.matmul(p_out[m][:, :], shared_dn[:, m * P:(m + 1) * P],
                                   shared_up, start=False, stop=False)
                mm.then_inc(S["sh_down"], 1)

            def out_proj(m):
                def product(ch):
                    for g in range(G):
                        pe.wait_ge(S["yz"], ONE + G * (ch.c - 1) + g + 1)
                        mm = pe.matmul(p_side[:, :], out_wT[:, g, m * P:(m + 1) * P], z_gate[:, g, :],
                                       start=(g == 0), stop=(g == G - 1))
                    return mm
                return product

            def transpose_x(k):
                def product(ch):
                    for t in range(TT):
                        pe.wait_ge(S["xn"], ONE + TT * (ch.c + 1) + t + 1)
                        mm = pe.transpose(p_side[:, t * P:(t + 1) * P], x_ln[:, t, k * P:(k + 1) * P], ident[:, :])
                    return mm
                return product

            def tokens(q):
                def product(ch):
                    pe.wait_ge(s_read, ONE + ch.fill("out_proj1"))
                    for t in range(2):
                        for m in range(KM):
                            mm = pe.transpose(p_side[:, t * DM + m * P:t * DM + (m + 1) * P],
                                              o_sb[:, m, (2 * q + t) * P:(2 * q + t + 1) * P], ident[:, :])
                    return mm
                return product

            def in_proj(m, other_half):
                def product(ch):
                    tokens_T = xnT[ch.next_place()[1] if other_half else ch.half]
                    return in_parts(p_side, [(in_w[:, :, k, m * P:(m + 1) * P], tokens_T[:, :, k, :])
                                             for k in range(KM)])
                return product

            def shared(i):
                def product(ch):
                    return in_parts(p_side, [(shared_gu[:, :, (2 * i + k) * NI:(2 * i + k + 1) * NI],
                                              xnT[ch.half][:, :, k, :]) for k in range(KM)])
                return product

            def router(ch):
                half = ch.next_place()[1]
                for t in range(TT):
                    out = p_side[:, t * NE:(t + 1) * NE]
                    for k in range(KM):
                        for part in range(PARTS):
                            pe.matmul(out, xnT[half][:, part, k, t * P:(t + 1) * P].bitcast(F32), router_w[:, k, :],
                                      start=(k == 0 and part == 0), stop=False)
                    mm = pe.matmul(out, ones_row[:, :], router_b[:, :], start=False, stop=True)
                return mm

            def b_and_c(ch):
                for g in range(G):
                    pe.wait_ge(S["xs2"], ONE + G * (ch.c + 1) + g + 1)
                    mm = pe.matmul(p_side[0:2 * NS, :], bc_wT[:, g, :], xs2[:, g, :],
                                   start=(g == 0), stop=(g == G - 1))
                return mm

            def dt_proj(m):
                def product(ch):
                    for g in range(G):
                        mm = pe.matmul(p_side[:, :], dt_fused[:, g, m * P:(m + 1) * P], xs2[:, g, :],
                                       start=(g == 0), stop=(g == G - 1))
                    return mm
                return product

            def weights(ch):
                pe.wait_ge(S["weight_lo"], ONE + ch.c + 2)
                apart(pe)
                for t in range(TT):
                    mm = pe.transpose(p_side[0:2 * NE, t * P:(t + 1) * P],
                                      weight_split[:, t, :, :].bitcast(F32).rearrange("p a e -> p (a e)"),
                                      ident[:, :])
                return mm

            products = {
                "out_proj0": out_proj(0), "out_proj1": out_proj(1), "xnT0": transpose_x(0), "xnT1": transpose_x(1),
                "logits": router, "tokens0": tokens(0), "tokens1": tokens(1), "shared_gate": shared(0),
                "shared_up": shared(1), "bc": b_and_c, "weights": weights,
                **{f"x{g}": in_proj(g, True) for g in range(G)}, **{f"z{g}": in_proj(G + g, False) for g in range(G)},
                **{f"dt{g}": dt_proj(g) for g in range(G)},
            }
            table = {at: [(kind, fill(name, products[name]))] for at, (kind, name) in FILLS.items()}
            table[(3, "A")] += [("once", fuse), ("once", constants)]
            table[(9, "A")].append(("once", fused))
            table[(0, "down")] = [("own", biases)]
            table[(SHARED_DOWN_STEP, "A")] = [("own", shared_down)]

            def sides(ch):
                alone(table)(ch)
                if ch is start:
                    pe.wait_ge(s_row_b0, ONE + 16)
                    pe.matmul(p_bc[:, :], pick[0:2, 0, :], row_b0[:, :], start=True, stop=True).then_inc(s_b, 1)

            def steps(ch):
                for s in range(NS):
                    n, k = ch.c * NS + s, s % 2
                    turn = ch.c * (NS // 2) + s // 2
                    ahead_half = ch.half if s + 1 < NS else ch.next_place()[1]
                    more = s + 1 < NS or "pre" in ch.kinds

                    def gate(n, k, half, j):
                        pe.wait_ge(s_gate_in, ONE + EN * n + j)
                        in_parts(p_gate, [(w_gu[k][:, :, j, kk * NI:(kk + 1) * NI], xnT[half][:, :, kk, :])
                                          for kk in range(KM)]).then_inc(s_gate, 1)

                    def up(n, k, half, j):
                        pe.wait_ge(s_act_up, ONE + EN * n + j)
                        in_parts(p_up, [(w_gu[k][:, :, j, (KM + kk) * NI:(KM + kk + 1) * NI],
                                         xnT[half][:, :, kk, :]) for kk in range(KM)]).then_inc(s_up, 1)

                    def spread_weight(j):
                        pe.wait_ge(s_hidden, ONE + EN * n + j)
                        pe.matmul(p_w[:, :], pick[:, 2 + j, :], rows[k][:, :], start=True, stop=True)\
                          .then_inc(s_wb, 1)

                    def down(n, k, j, last=False):
                        pe.wait_ge(s_hid_lo, ONE + EN * n + j + 1)
                        for m in range(KM):
                            for part, hid in ((0, hid_hi[j]), (0, hid_lo[j]), (1, hid_hi[j])):
                                mm = pe.matmul(p_out[m][:, :], w_dn[k][:, part, j, m * P:(m + 1) * P], hid[:, :],
                                               start=False, stop=(last and part == 1))
                        mm.then_inc(s_down, 1)

                    def next_b():
                        pe.wait_ge(s_hc, ONE + n + 1)
                        if s < NS - 1 or not more:
                            pe.matmul(p_bc[:, :], pick[:, 0, :], rows[k][:, :], start=True, stop=True)\
                              .then_inc(s_b, 1)
                        else:
                            pe.wait_ge(s_row_b0, ONE + 16 * (ch.c + 2))
                            pe.matmul(p_bc[:, :], pick[0:2, 0, :], row_b0[:, :], start=True, stop=True)\
                              .then_inc(s_b, 1)

                    very_first = ch is first_chunk and s == 0
                    if very_first:
                        pe.wait_ge(s_gu_lo, 1)
                        gate(n, k, ch.half, 0)
                        up(n, k, ch.half, 0)
                        gate(n, k, ch.half, 1)
                    pe.wait_ge(s_rows[k], ONE + 16 * (turn + 1))
                    spread_weight(0)
                    pe.wait_ge(s_u_in, ONE + 2 * (n + 1))
                    pe.matmul(p_bc[:, :], pick[:, 1, :], rows[k][:, :], start=True, stop=True).then_inc(s_c, 1)
                    up(n, k, ch.half, 1)
                    if not very_first:
                        down(n - 1, 1 - k, 1, last=(s == 0))
                    spread_weight(1)
                    beside(table, ch, s, "A")
                    if crowded(ch, s):
                        next_b()
                    if more:
                        if ch is first_chunk and s + 1 < NS:
                            pe.wait_ge(s_gu_lo, s + 2)
                        else:
                            pe.wait_ge(s_wgu[1 - k], ONE + 16 * (ch.c * (NS // 2) + (s + 1) // 2 + 1 - NS // 2))
                        gate(n + 1, 1 - k, ahead_half, 0)
                    if not crowded(ch, s):
                        next_b()
                    if more:
                        up(n + 1, 1 - k, ahead_half, 0)
                        gate(n + 1, 1 - k, ahead_half, 1)
                    beside(table, ch, s, "down")
                    if ch is first_chunk:
                        pe.wait_ge(s_dn_lo, s + 1)
                    else:
                        pe.wait_ge(s_wdn[k], ONE + 16 * (turn + 1 - NS // 2))
                    down(n, k, 0)
                    beside(table, ch, s, "B")
                    if not more:
                        down(n, k, 1, last=True)

            all_chunks(pe, sides, steps)


def kernel(**inputs):
    import numpy as np
    import concourse.bacc as bacc
    from concourse.bass_utils import run_bass_kernel_spmd

    a = {k.split("_", 2)[2]: np.asarray(v) for k, v in inputs.items()}

    def blocks(w):
        return w.reshape(w.shape[0] // P, P, -1).transpose(1, 0, 2)

    def columns(v):
        return v.reshape(-1, P).T

    def expert(gate, up, down):
        lead = gate.shape[:-2]
        parts = [w.reshape(*lead, KM, P, NI)[..., k, :, :] for w in (gate, up) for k in range(KM)]
        return np.concatenate(parts, axis=-1), down

    x_proj = a["x_proj_w"]
    turned = np.roll(np.arange(NS), -1)
    bc = np.concatenate([x_proj[DI:DI + NS][turned], x_proj[DI + NS:]], axis=0)
    gu, dn = expert(a["Wg"], a["Wu"], a["Wd"])
    pairs = np.arange(NE).reshape(EN, NS).T
    gu_s, dn_s = expert(a["Wg_s"], a["Wu_s"], a["Wd_s"])
    order = pairs.reshape(-1)
    arrays = {
        "x": a["x"],
        "in_wT": blocks(a["in_proj_w"].T), "bc_wT": blocks(bc.T), "out_wT": blocks(a["out_proj_w"].T),
        "x_w": blocks(x_proj[:DI]), "dt_wT": blocks(a["dt_proj_w"].T),
        "shared_w": np.concatenate([gu_s, dn_s], axis=-1),
        "router_w": blocks(a["Wr"]), "router_b": a["br"].reshape(1, NE),
        "down_b": a["bd"], "shared_down_b": columns(a["bd_s"]),
        "conv_w": blocks(a["conv_w"].reshape(DI, TAPS)), "conv_b": columns(a["conv_b"]),
        "dt_b": columns(a["dt_proj_b"]), "skip_d": columns(a["D"]),
        "a_log": blocks(a["A_log"]).transpose(0, 2, 1).reshape(P, NS * G),
        "gate_b": np.concatenate([a["bg"][order], a["bg_s"].reshape(1, NI)]).T,
        "up_b": np.concatenate([a["bu"][order], a["bu_s"].reshape(1, NI)]).T,
        "w_gu": gu[pairs].transpose(0, 2, 1, 3), "w_dn": dn[pairs].transpose(0, 2, 1, 3),
        "ident": np.eye(P, dtype=np.float32),
        "pick": np.repeat(np.repeat(np.eye(ROWS // 2, dtype=np.float32), 2, axis=0)[:, :, None], P, axis=2),
    }
    nc = bacc.Bacc("TRN2", target_bir_lowering=False, num_devices=1)
    feed, io = {}, {}
    for name, v in arrays.items():
        v = np.ascontiguousarray(v)
        feed[f"in_{name}"] = v
        io[name] = nc.dram_tensor(f"in_{name}", v.shape, mybir.dt.from_np(v.dtype), kind="ExternalInput").ap()
    io["out"] = nc.dram_tensor("out_y", (BATCH, SEQ, DM), F32, kind="ExternalOutput").ap()
    build_program(nc, io)
    result = run_bass_kernel_spmd(nc, [feed], core_ids=[0])
    return result.results[0]["out_y"]
```
